# Optimizing a Trainium2 kernel written in Bass

```python
import numpy as np
import jax
import jax.numpy as jnp

def _softmax(x, axis=-1):
    return jax.nn.softmax(x, axis=axis)

def _gelu(x):
    return jax.nn.gelu(x, approximate=True)

def _silu(x):
    return jax.nn.silu(x)

def _sigmoid(x):
    return jax.nn.sigmoid(x)

def _layernorm(x, axis=-1, eps=1e-05):
    m = jnp.mean(x, axis=axis, keepdims=True)
    v = jnp.var(x, axis=axis, keepdims=True)
    return (x - m) / jnp.sqrt(v + eps)

def _scatter_add(tgt, idx, src, axis=0):
    return tgt.at[idx].add(src)

def _segment_sum(src, seg, n):
    return jax.ops.segment_sum(src, seg, n)
kernel_name = 'mk_flamingo_gated_d1_seqx_r4_bcc993'

def setup_inputs(seed: int=0):
    np.random.seed(seed)
    _w = jnp.asarray

    def _rec_inputs():
        import jax
        import jax.numpy as jnp
        _rk = jax.random.key(seed)
        x = -0.000125 + 0.9999 * jax.random.normal(jax.random.fold_in(_rk, 1), (4, 512, 512), jnp.float32)
        _lenS = 512 - jax.random.randint(jax.random.fold_in(_rk, 7), (4,), 0, max(1, 512 // 4) + 1, jnp.int32)
        _lenS2 = 512 - jax.random.randint(jax.random.fold_in(_rk, 8), (4,), 0, max(1, 512 // 4) + 1, jnp.int32)
        fside_BxS2xS2_0 = -3.05549e-07 + 0.0199987 * jax.random.normal(jax.random.fold_in(_rk, 11), (4, 512, 512), jnp.float32)
        _ctx_1024P = jax.random.normal(jax.random.fold_in(_rk, 12), (4, 16, 256), jnp.float32)
        _ctx_1024c = jax.random.dirichlet(jax.random.fold_in(_rk, 512), 0.3 * jnp.ones((16,), jnp.float32), (4, 512))
        _ctx_1024t = jnp.einsum('bsk,bkd->bsd', _ctx_1024c, _ctx_1024P)
        _ctx_1024t = _ctx_1024t * jax.lax.rsqrt(jnp.mean(jnp.square(_ctx_1024t)) + 1e-12) * 0.953939
        ctx_1024 = 6.82029e-06 + 0.0200006 * (_ctx_1024t + 0.3 * jax.random.normal(jax.random.fold_in(_rk, 612), (4, 512, 256), jnp.float32))
        _g = jax.random.normal(jax.random.fold_in(_rk, 9001), (2, 1), jnp.float32)
        _g = jnp.sign(_g) * jnp.maximum(jnp.abs(_g), 1.0) + (_g == 0) * 1.0
        g_xattn = _g[0]
        g_ffn = _g[1]
        return (x, fside_BxS2xS2_0, ctx_1024, g_xattn, g_ffn)
    x, fside_BxS2xS2_0, ctx_1024, g_xattn, g_ffn = _rec_inputs()

    def _L0_xattn_setup():
        import jax, jax.numpy as jnp
        import numpy as np
        EPS = 1e-06
        QMAX = 127.0

        def _smooth_quant_linear(x, w):
            amax_x = jnp.max(jnp.abs(x), axis=0)
            amax_w = jnp.max(jnp.abs(w), axis=0)
            s = jnp.sqrt(jnp.maximum(amax_x, EPS) / jnp.maximum(amax_w, EPS))
            s = jnp.maximum(s, EPS)
            xs = x / s
            ws = w * s
            x_scale = jnp.maximum(jnp.max(jnp.abs(xs), axis=-1, keepdims=True), EPS) / QMAX
            w_scale = jnp.maximum(jnp.max(jnp.abs(ws), axis=-1, keepdims=True), EPS) / QMAX
            x_q = jnp.clip(jnp.round(xs / x_scale), -QMAX, QMAX)
            w_q = jnp.clip(jnp.round(ws / w_scale), -QMAX, QMAX)
            return x_q @ w_q.T * x_scale * w_scale.T

        def _expert_forward(xe, guw, dw):
            h = _smooth_quant_linear(xe, guw)
            gate, up = jnp.split(h, 2, axis=-1)
            a = jax.nn.silu(gate) * up
            return _smooth_quant_linear(a, dw)
        key = jax.random.key(seed)
        k1, k2, k3 = jax.random.split(key, 3)
        E, T, D, I = (8, 512, 512, 256)
        x = jax.random.normal(k1, (E, T, D), dtype=jnp.float32)
        gate_up_weight = jax.random.normal(k2, (E, 2 * I, D), dtype=jnp.float32) * 0.02
        down_weight = jax.random.normal(k3, (E, D, I), dtype=jnp.float32) * 0.02
        return {'x': x, 'gate_up_weight': gate_up_weight, 'down_weight': down_weight}
    _L0_xattn_all = _L0_xattn_setup()
    _L0_xattn_in = {k: v for k, v in _L0_xattn_all.items() if k in ()}
    del _L0_xattn_all

    def _L0_ffn_setup():
        import jax, jax.numpy as jnp
        import numpy as np
        TOP_K = 2
        key = jax.random.key(seed)
        ks = jax.random.split(key, 5)
        B, S, D, M, E = (4, 512, 512, 512, 8)
        x = jax.random.normal(ks[0], (B, S, D), dtype=jnp.float32)
        gate_kernel = jax.random.normal(ks[1], (D, E), dtype=jnp.float32) / np.sqrt(D)
        wi_0 = jax.random.normal(ks[2], (E, D, M), dtype=jnp.float32) / np.sqrt(D)
        wi_1 = jax.random.normal(ks[3], (E, D, M), dtype=jnp.float32) / np.sqrt(D)
        wo = jax.random.normal(ks[4], (E, M, D), dtype=jnp.float32) / np.sqrt(M)
        return {'x': x, 'gate_kernel': gate_kernel, 'wi_0': wi_0, 'wi_1': wi_1, 'wo': wo}
    _L0_ffn_all = _L0_ffn_setup()
    _L0_ffn_in = {k: v for k, v in _L0_ffn_all.items() if k in ('gate_kernel', 'wi_0', 'wi_1', 'wo')}
    del _L0_ffn_all
    return {'x': x, 'fside_BxS2xS2_0': fside_BxS2xS2_0, 'ctx_1024': ctx_1024, 'g_xattn': g_xattn, 'g_ffn': g_ffn, 'L0_ffn_gate_kernel': _L0_ffn_in['gate_kernel'], 'L0_ffn_wi_0': _L0_ffn_in['wi_0'], 'L0_ffn_wi_1': _L0_ffn_in['wi_1'], 'L0_ffn_wo': _L0_ffn_in['wo']}

def reference(x, fside_BxS2xS2_0, ctx_1024, g_xattn, g_ffn, L0_ffn_gate_kernel, L0_ffn_wi_0, L0_ffn_wi_1, L0_ffn_wo):
    import jax
    import jax.numpy as jnp

    def _L0_xattn_ref(x, gate_up_weight, down_weight):
        import jax, jax.numpy as jnp
        import numpy as np
        EPS = 1e-06
        QMAX = 127.0

        def _smooth_quant_linear(x, w):
            amax_x = jnp.max(jnp.abs(x), axis=0)
            amax_w = jnp.max(jnp.abs(w), axis=0)
            s = jnp.sqrt(jnp.maximum(amax_x, EPS) / jnp.maximum(amax_w, EPS))
            s = jnp.maximum(s, EPS)
            xs = x / s
            ws = w * s
            x_scale = jnp.maximum(jnp.max(jnp.abs(xs), axis=-1, keepdims=True), EPS) / QMAX
            w_scale = jnp.maximum(jnp.max(jnp.abs(ws), axis=-1, keepdims=True), EPS) / QMAX
            x_q = jnp.clip(jnp.round(xs / x_scale), -QMAX, QMAX)
            w_q = jnp.clip(jnp.round(ws / w_scale), -QMAX, QMAX)
            return x_q @ w_q.T * x_scale * w_scale.T

        def _expert_forward(xe, guw, dw):
            h = _smooth_quant_linear(xe, guw)
            gate, up = jnp.split(h, 2, axis=-1)
            a = jax.nn.silu(gate) * up
            return _smooth_quant_linear(a, dw)
        return jax.vmap(_expert_forward)(x, gate_up_weight, down_weight)

    def _L0_ffn_ref(x, gate_kernel, wi_0, wi_1, wo):
        import jax, jax.numpy as jnp
        import numpy as np
        TOP_K = 2
        E = gate_kernel.shape[-1]
        gate_logits = jnp.einsum('bsd,de->bse', x, gate_kernel)
        top_k_weights, top_k_indices = jax.lax.top_k(gate_logits, TOP_K)
        top_k_weights = jax.nn.softmax(top_k_weights.astype(jnp.float32), axis=-1).astype(x.dtype)
        combine_w = jnp.sum(jax.nn.one_hot(top_k_indices, E, dtype=x.dtype) * top_k_weights[..., None], axis=-2)
        h0 = jnp.einsum('bsd,edm->bsem', x, wi_0)
        h1 = jnp.einsum('bsd,edm->bsem', x, wi_1)
        h = jax.nn.silu(h0) * h1 * combine_w[..., None]
        out = jnp.einsum('bsem,emd->bsd', h, wo)
        return out
    x = x + jnp.tanh(g_xattn[0]) * _L0_xattn_ref(_layernorm(x, axis=-1), fside_BxS2xS2_0, ctx_1024)
    x = x + jnp.tanh(g_ffn[0]) * _L0_ffn_ref(_layernorm(x, axis=-1), L0_ffn_gate_kernel, L0_ffn_wi_0, L0_ffn_wi_1, L0_ffn_wo)
    return x

_drawn_inputs = setup_inputs


def setup_inputs(seed=0):
    import zlib

    import numpy as np

    out = dict(_drawn_inputs(seed))
    spreads = {}
    factors = {}
    for name, (base, spread) in spreads.items():
        noise = np.random.default_rng([zlib.crc32(name.encode()), seed]).standard_normal(out[name].shape)
        drawn = base * np.exp(spread * noise) if base else spread * noise
        out[name] = jnp.asarray(drawn.astype(out[name].dtype))
    for name, factor in factors.items():
        out[name] = (out[name] * factor).astype(out[name].dtype)
    return out
```

```python
import concourse.bass as bass
from concourse import mybir
from concourse.alu_op_type import AluOpType as ALU
from contextlib import ExitStack

F32, BF16, F16 = mybir.dt.float32, mybir.dt.bfloat16, mybir.dt.float16
I32, U32 = mybir.dt.int32, mybir.dt.uint32
ACT = mybir.ActivationFunctionType
AX = mybir.AxisListType

P = 128
B, T, D = 4, 512, 512
I = 256
E, M, TOPK = 8, 512, 2
TJ = T // P
DC, IC, MC = D // P, I // P, M // P
NT = B * TJ
SLOT_TILES = B * T * TOPK // P + E - 1
IDX_COLS = SLOT_TILES + 1
ROW = D + E
EPS_Q, QMAX, EPS_LN = 1e-6, 127.0, 1e-5
MAGIC = 1.5 * 2.0 ** 23
KW = 3 * DC * M


def program(nc, x, guw, dw, g_xattn, g_ffn, gate_kernel, wi_0, wi_1, wo, out):
    rows = nc.dram_tensor("token_rows", [B * T, ROW], F32, kind="Internal").ap()
    x_v = x.rearrange("b (j p) d -> b p j d", p=P)
    guw_v = guw.rearrange("b (r p) d -> b p r d", p=P)
    dw_v = dw.rearrange("b (r p) i -> b p r i", p=P)
    out_rows = out.rearrange("b t d -> (b t) d")
    out_v = out_rows.rearrange("(n p) d -> p n d", p=P)
    rows_v = rows.rearrange("(n p) c -> p n c", p=P)
    expert_v = [w.rearrange("e (c p) n -> e p c n", p=P) for w in (wi_0, wi_1, wo)]

    ctx = ExitStack()
    with ctx:
        def sb(name, shape, dt):
            return ctx.enter_context(nc.sbuf_tensor(name, shape, dt))

        def pb(name, shape, dt=F32):
            return ctx.enter_context(nc.psum_tensor(name, shape, dt))

        def sem(name):
            return ctx.enter_context(nc.semaphore(name))

        experts = sb("experts", [P, E, 3 * DC, M], F32)
        flat = experts[:].rearrange("p e k n -> p (e k n)")
        first_words = 3 * KW
        first_at = E * KW - first_words
        cursor = [first_at]

        def early(words):
            at = cursor[0]
            cursor[0] += words
            assert cursor[0] <= E * KW
            return flat[:, at:at + words]

        X = early(NT * D).rearrange("p (n d) -> p n d", d=D)
        XN = early(TJ * D).rearrange("p (j d) -> p j d", d=D)
        TQ = early(8 * D).rearrange("p (k d) -> p k d", d=D)
        W1 = early(TJ * D).rearrange("p (r d) -> p r d", d=D)
        w1qT = early(DC * T // 2).bitcast(BF16).rearrange("p (c o) -> p c o", c=DC)
        xqT = early(DC * T // 2).bitcast(BF16).rearrange("p (c t) -> p c t", c=DC)
        TQ2 = TQ[:, 4:8, :].rearrange("p k d -> p (k d)").rearrange("p (k i) -> p k i", i=I)

        region = sb("region", [P, 5120], F32)

        def part(at, words):
            return region[:, at:at + words]

        W2 = part(0, 1024).rearrange("p (r i) -> p r i", i=I)
        A = part(1024, 1024).rearrange("p (j i) -> p j i", i=I)
        w2qT = part(2048, 512).bitcast(BF16).rearrange("p (c o) -> p c o", c=IC)
        aqT = part(2560, 512).bitcast(BF16).rearrange("p (c t) -> p c t", c=IC)
        w1_scale_row = part(3072, 512)
        w2_scale_row = part(3584, 512)
        xn2T = part(4096, 1024).rearrange("p (s c t) -> p s c t", s=2, c=DC)
        onehot_b = part(0, 2048).bitcast(F16).rearrange("p (s n b) -> p s n b", s=2, n=NT)
        onehot_a = part(2048, 1024).bitcast(F16).rearrange("p (e n a) -> p e n a", e=E, n=NT)
        rt = [part(3072 + 128 * k, 128).rearrange("p (e n) -> p e n", e=E) for k in range(14)]
        G = part(0, ROW)
        XT = part(528, 512).rearrange("p (c s) -> p c s", c=DC)
        SIL = part(1040, 512)
        HH = part(1552, 512).rearrange("p (c s) -> p c s", c=MC)
        HT = part(2064, 512).rearrange("p (c s) -> p c s", c=MC)
        YS = part(2576, 512)
        cwm = part(3088, E)
        cw_tile = part(3100, 1)

        ident = sb("ident", [P, P], F32)
        upper = sb("upper", [P, P], BF16)
        ones = sb("ones", [P, P], BF16)
        gate_sb = sb("gate_sb", [P, DC, E], F32)
        bst = sb("bst", [P, TJ, 6], F32)
        mv = sb("mv", [P, TJ, 2], F32)
        var_eps = sb("var_eps", [P, TJ], F32)
        sd = sb("sd", [P, TJ], F32)
        rstd = sb("rstd", [P, TJ], F32)
        amax = sb("amax", [P, 8], F32)
        amax_c = sb("amax_c", [P, 8], F32)
        amax_r = sb("amax_r", [P, 4], F32)
        ratio = sb("ratio", [P, 4], F32)
        smooth = sb("smooth", [P, 2, 4], F32)
        rowmax = sb("rowmax", [P, 8], F32)
        qscale = sb("qscale", [P, 2, 8], F32)
        qinv = sb("qinv", [P, 8], F32)
        gates = sb("gates", [P, 2], F32)
        tanh_g = sb("tanh_g", [P, 2], F32)
        logits = sb("logits", [P, NT, E], F32)
        top = sb("top", [P, NT, 8], F32)
        top_i = sb("top_i", [P, NT, 8], U32)
        n_e = sb("n_e", [P, 4, E], F32)
        n_i = sb("n_i", [P, 2, E], I32)
        iota_e = sb("iota_e", [P, E], F32)
        iota_a = sb("iota_a", [P, 16], F32)
        iota_b = sb("iota_b", [P, P], F32)
        iota_p = sb("iota_p", [P, 1], F32)
        tidx = sb("tidx", [P, NT], F32)
        tm = sb("tm", [P, 6, IDX_COLS], F32)
        slot_expert = sb("slot_expert", [P, IDX_COLS], I32)
        slot_token = sb("slot_token", [P, IDX_COLS], I32)
        slot_onehot = sb("slot_onehot", [P, IDX_COLS, E], F32)
        idx_gather = sb("idx_gather", [P, 1], I32)
        idx_scatter = sb("idx_scatter", [P, 1], I32)

        TV = [pb(f"TV{k}", [P, 512]) for k in range(2)]
        TA = [pb(f"TA{k}", [P, 512]) for k in range(2)]
        RB = [pb(f"RB{k}", [P, 512]) for k in range(2)]
        AC = [pb(f"AC{k}", [P, 512]) for k in range(2)]

        names = """consts_ready ident_zero gates_in gate_in x_in w1_in w2_in experts_in tanh_ready
            x_out_done rows_done weights_out_done
            stats mean var_ready sd_ready rstd_ready xn_ready
            tv_full tv_free ta_full ta_free ac_full ac_free
            amax1 amax2 ratio_ready smooth_sqrt smooth_ready rows_ready w1_used w2_used
            scaled rowmax_done qscale_ready magic_ready clip_ready
            magic2_ready clip2_ready qT_ready qT2_ready scale_row_full scale_row_ready
            h_ready silu_ready a_ready o_ready x2_ready
            stats2 var2_ready sd2_ready rstd2_ready xn2_ready xn2T_ready
            v_chain exp_ready cw_row_ready mask_ready counts_full onehot_ready onehot_used
            table_sb tableT_full tableT_sb slots_full slots_ready p_chain p_passed v_passed
            gathered gather_used xT_full xT_ready h0_full h1_full sil_ready hh_ready hT_full hT_ready
            y_full ys_ready cw_ready scattered ys_free""".split()
        S = {n: sem(n) for n in names}
        block = ctx.enter_context(nc.Block())

        def cols(ap, n):
            return ap.unsqueeze(2).to_broadcast([P, ap.shape[1], n])

        @block.sync
        def _(sp):
            sp.dma_start(X[:, 0:TJ, :], x_v[0]).then_inc(S["x_in"], 16)
            sp.dma_start(W1, guw_v[0]).then_inc(S["w1_in"], 16)
            sp.dma_start(W2, dw_v[0]).then_inc(S["w2_in"], 16)
            sp.dma_start(gates[:, 0:1], g_xattn.unsqueeze(0).to_broadcast([P, 1])).then_inc(S["gates_in"], 16)
            sp.dma_start(gates[:, 1:2], g_ffn.unsqueeze(0).to_broadcast([P, 1])).then_inc(S["gates_in"], 16)
            sp.dma_start(gate_sb[:], gate_kernel.rearrange("(c p) e -> p c e", p=P)).then_inc(S["gate_in"], 16)
            for b in range(1, B):
                sp.wait_ge(S["x_in"], 16 * b)
                sp.dma_start(X[:, b * TJ:(b + 1) * TJ, :], x_v[b]).then_inc(S["x_in"], 16)
            for b in range(B):
                if b + 1 < B:
                    sp.wait_ge(S["w1_used"], b + 1)
                    sp.dma_start(W1, guw_v[b + 1]).then_inc(S["w1_in"], 16)
                    sp.wait_ge(S["w2_used"], b + 1)
                    sp.dma_start(W2, dw_v[b + 1]).then_inc(S["w2_in"], 16)
                for k in range(3):
                    sp.dma_start(experts[:, b, k * DC:(k + 1) * DC, :], expert_v[k][b]).then_inc(S["experts_in"], 16)
                sp.wait_ge(S["x2_ready"], TJ * (b + 1))
                sp.dma_start(out_v[:, b * TJ:(b + 1) * TJ, :], X[:, b * TJ:(b + 1) * TJ, :]).then_inc(S["x_out_done"], 16)
                sp.wait_ge(S["xn2_ready"], TJ * (b + 1))
                sp.dma_start(rows_v[:, b * TJ:(b + 1) * TJ, 0:D], XN).then_inc(S["rows_done"], 16)
            for k in range(3):
                sp.dma_start(experts[:, B, k * DC:(k + 1) * DC, :], expert_v[k][B]).then_inc(S["experts_in"], 16)
            sp.wait_ge(S["x_out_done"], 16 * B)
            sp.wait_ge(S["rows_done"], 16 * B)
            sp.wait_ge(S["ac_free"], 2 + 12 * B)
            for e in range(B + 1, E):
                for k in range(3):
                    sp.dma_start(experts[:, e, k * DC:(k + 1) * DC, :], expert_v[k][e]).then_inc(S["experts_in"], 16)
            sp.wait_ge(S["cw_row_ready"], 1)
            sp.dma_start(rows_v[:, :, D:ROW], top[:]).then_inc(S["weights_out_done"], 16)

        @block.vector
        def _(dve):
            V = nc.vector
            chain = [0]

            def link(ins):
                chain[0] += 1
                ins.then_inc(S["v_chain"], 1)
                dve.wait_ge(S["v_chain"], chain[0])

            dve.sem_inc(S["tv_free"], 2)
            dve.sem_inc(S["ac_free"], 2)
            dve.wait_ge(S["consts_ready"], 1)
            n_chain = 15
            with dve.Fori(0, B) as b:
                def linkb(k, ins):
                    ins.then_inc(S["v_chain"], 1)
                    dve.wait_ge(S["v_chain"], b * n_chain + k)

                def tile(j):
                    return X[:, bass.ds(b * TJ + j, 1), :].rearrange("p a d -> p (a d)")

                dve.wait_ge(S["x_in"], b * 16 + 16)
                dve.sem_inc(S["v_passed"], 1)
                for j in range(TJ):
                    last = V.bn_stats(bst[:, j, :], tile(j))
                linkb(1, last)
                dve.sem_inc(S["v_passed"], 1)
                for j in range(TJ):
                    last = V.bn_aggr(mv[:, j, :], bst[:, j, :])
                linkb(2, last)
                V.tensor_scalar(var_eps[:], mv[:, :, 1], EPS_LN, None, ALU.add).then_inc(S["var_ready"], 1)
                for c in range(DC):
                    dve.wait_ge(S["tv_full"], b * 12 + c + 1)
                    V.tensor_reduce(amax[:, c:c + 1], TV[c % 2][:], axis=AX.X, op=ALU.max,
                                    apply_absolute_value=True).then_inc(S["tv_free"], 1)
                dve.wait_ge(S["sd_ready"], b + 1)
                linkb(3, V.reciprocal(rstd[:], sd[:]))
                for j in range(TJ):
                    V.tensor_scalar(XN[:, j, :], tile(j), mv[:, j, 0:1], rstd[:, j:j + 1],
                                    ALU.subtract, ALU.mult).then_inc(S["xn_ready"], 1)
                for c in range(DC):
                    dve.wait_ge(S["tv_full"], b * 12 + DC + c + 1)
                    last = V.tensor_reduce(amax[:, 4 + c:5 + c], TV[c % 2][:], axis=AX.X, op=ALU.max,
                                           apply_absolute_value=True)
                    last.then_inc(S["tv_free"], 1)
                dve.wait_ge(S["tv_free"], b * 12 + 2 * DC + 2)
                linkb(4, V.tensor_scalar(amax_c[:], amax[:], EPS_Q, None, ALU.max))
                linkb(5, V.reciprocal(amax_r[:], amax_c[:, 0:4]))
                V.tensor_tensor(ratio[:], amax_c[:, 4:8], amax_r[:], ALU.mult).then_inc(S["ratio_ready"], 1)
                dve.wait_ge(S["smooth_sqrt"], b * 2 + 1)
                linkb(6, V.tensor_scalar(smooth[:, 0, :], smooth[:, 0, :], EPS_Q, None, ALU.max))
                V.reciprocal(smooth[:, 1, :], smooth[:, 0, :]).then_inc(S["smooth_ready"], 1)
                dve.wait_ge(S["rows_ready"], b * 4 + 1)
                for j in range(TJ):
                    last = V.tensor_tensor(TQ[:, j, :], W1[:, j, :], RB[0][:], ALU.mult)
                last.then_inc(S["w1_used"], 1)
                dve.wait_ge(S["rows_ready"], b * 4 + 2)
                for j in range(TJ):
                    last = V.tensor_tensor(TQ[:, 4 + j, :], XN[:, j, :], RB[1][:], ALU.mult)
                linkb(7, last)
                last = V.tensor_reduce(rowmax[:], TQ, axis=AX.X, op=ALU.max, apply_absolute_value=True)
                linkb(8, last)
                linkb(9, V.tensor_scalar(qscale[:, 0, :], rowmax[:], EPS_Q, 1.0 / QMAX, ALU.max, ALU.mult))
                V.reciprocal(qinv[:], qscale[:, 0, :]).then_inc(S["qscale_ready"], 1)
                for k in range(8):
                    dve.wait_ge(S["magic_ready"], b * 8 + k + 1)
                    V.tensor_scalar(TQ[:, k, :], TQ[:, k, :], MAGIC - QMAX, MAGIC + QMAX,
                                    ALU.max, ALU.min).then_inc(S["clip_ready"], 1)
                dve.wait_ge(S["scale_row_ready"], b * 2 + 1)
                for j in range(TJ):
                    dve.wait_ge(S["ac_full"], b * 12 + j + 1)
                    V.scalar_tensor_tensor(TQ[:, j, :], AC[j % 2][:], qscale[:, 0, 4 + j:5 + j], w1_scale_row,
                                           ALU.mult, ALU.mult).then_inc(S["h_ready"], 1)
                    dve.wait_ge(S["h_ready"], b * 4 + j + 1)
                    V.sem_inc(S["ac_free"], 1)
                for c in range(IC):
                    dve.wait_ge(S["tv_full"], b * 12 + 2 * DC + c + 1)
                    V.tensor_reduce(amax[:, c:c + 1], TV[c % 2][:], axis=AX.X, op=ALU.max,
                                    apply_absolute_value=True).then_inc(S["tv_free"], 1)
                for c in range(IC):
                    dve.wait_ge(S["tv_full"], b * 12 + 2 * DC + IC + c + 1)
                    last = V.tensor_reduce(amax[:, 4 + c:5 + c], TV[c % 2][:], axis=AX.X, op=ALU.max,
                                           apply_absolute_value=True)
                    last.then_inc(S["tv_free"], 1)
                dve.wait_ge(S["tv_free"], b * 12 + 12 + 2)
                linkb(10, V.tensor_scalar(amax_c[:], amax[:], EPS_Q, None, ALU.max))
                linkb(11, V.reciprocal(amax_r[:], amax_c[:, 0:4]))
                V.tensor_tensor(ratio[:], amax_c[:, 4:8], amax_r[:], ALU.mult).then_inc(S["ratio_ready"], 1)
                dve.wait_ge(S["smooth_sqrt"], b * 2 + 2)
                linkb(12, V.tensor_scalar(smooth[:, 0, :], smooth[:, 0, :], EPS_Q, None, ALU.max))
                V.reciprocal(smooth[:, 1, :], smooth[:, 0, :]).then_inc(S["smooth_ready"], 1)
                dve.wait_ge(S["rows_ready"], b * 4 + 3)
                for j in range(TJ):
                    last = V.tensor_tensor(TQ2[:, j, :], W2[:, j, :], RB[0][:, 0:I], ALU.mult)
                last.then_inc(S["w2_used"], 1)
                dve.wait_ge(S["rows_ready"], b * 4 + 4)
                for j in range(TJ):
                    last = V.tensor_tensor(TQ2[:, 4 + j, :], A[:, j, :], RB[1][:, 0:I], ALU.mult)
                linkb(13, last)
                last = V.tensor_reduce(rowmax[:], TQ2, axis=AX.X, op=ALU.max, apply_absolute_value=True)
                linkb(14, last)
                linkb(15, V.tensor_scalar(qscale[:, 1, :], rowmax[:], EPS_Q, 1.0 / QMAX, ALU.max, ALU.mult))
                V.reciprocal(qinv[:], qscale[:, 1, :]).then_inc(S["qscale_ready"], 1)
                for k in range(8):
                    dve.wait_ge(S["magic2_ready"], b * 8 + k + 1)
                    V.tensor_scalar(TQ2[:, k, :], TQ2[:, k, :], MAGIC - QMAX, MAGIC + QMAX,
                                    ALU.max, ALU.min).then_inc(S["clip2_ready"], 1)
                dve.wait_ge(S["scale_row_ready"], b * 2 + 2)
                for j in range(TJ):
                    dve.wait_ge(S["ac_full"], b * 12 + 4 + j + 1)
                    V.scalar_tensor_tensor(TQ[:, j, :], AC[j % 2][:], qscale[:, 1, 4 + j:5 + j], w2_scale_row,
                                           ALU.mult, ALU.mult).then_inc(S["o_ready"], 1)
                    dve.wait_ge(S["o_ready"], b * 4 + j + 1)
                    V.sem_inc(S["ac_free"], 1)
                    V.tensor_tensor(tile(j), tile(j), TQ[:, j, :], ALU.add).then_inc(S["x2_ready"], 1)
                for j in range(TJ):
                    dve.wait_ge(S["x2_ready"], b * 4 + j + 1)
                    dve.sem_inc(S["v_passed"], 1)
                    last = V.bn_stats(bst[:, j, :], tile(j))
                last.then_inc(S["stats2"], 1)
                dve.wait_ge(S["stats2"], b * 2 + 1)
                dve.sem_inc(S["v_passed"], 1)
                for j in range(TJ):
                    last = V.bn_aggr(mv[:, j, :], bst[:, j, :])
                last.then_inc(S["stats2"], 1)
                dve.wait_ge(S["stats2"], b * 2 + 2)
                V.tensor_scalar(var_eps[:], mv[:, :, 1], EPS_LN, None, ALU.add).then_inc(S["var2_ready"], 1)
                dve.wait_ge(S["sd2_ready"], b + 1)
                V.reciprocal(rstd[:], sd[:]).then_inc(S["rstd2_ready"], 1)
                dve.wait_ge(S["rstd2_ready"], b + 1)
                for j in range(TJ):
                    V.tensor_scalar(XN[:, j, :], tile(j), mv[:, j, 0:1], rstd[:, j:j + 1],
                                    ALU.subtract, ALU.mult).then_inc(S["xn2_ready"], 1)
                for j in range(TJ):
                    dve.wait_ge(S["ac_full"], b * 12 + 8 + j + 1)
                    V.tensor_copy(logits[:, bass.ds(b * TJ + j, 1), :].rearrange("p a e -> p (a e)"),
                                  AC[j % 2][:, 0:E]).then_inc(S["ac_free"], 1)
                dve.wait_ge(S["rows_done"], b * 16 + 16)
            dve.wait_ge(S["ac_free"], 2 + 12 * B)
            chain[0] = n_chain * B

            for n in range(NT):
                last = V.max(top[:, n, :], logits[:, n, :])
            link(last)
            for n in range(NT):
                last = V.max_index(top_i[:, n, :], top[:, n, :], logits[:, n, :])
            link(last)
            oh = [rt[k].rearrange("p e n -> p (e n)").rearrange("p (n e) -> p n e", e=E) for k in range(2)]
            choice = tm[:, 0, 0:2 * NT].rearrange("p (n k) -> p n k", k=2)
            diff, prob1, prob2, den = (tm[:, k, 0:NT] for k in (1, 2, 3, 4))
            link(V.tensor_copy(choice, top_i[:, :, 0:2]))
            iota_ne = iota_e[:].unsqueeze(1).to_broadcast([P, NT, E])
            V.tensor_tensor(oh[0], iota_ne, choice[:, :, 0:1].to_broadcast([P, NT, E]), ALU.is_equal)
            V.tensor_tensor(oh[1], iota_ne, choice[:, :, 1:2].to_broadcast([P, NT, E]), ALU.is_equal)
            V.tensor_tensor(diff, top[:, :, 1], top[:, :, 0], ALU.subtract).then_inc(S["x2_ready"], 1)
            mask16 = onehot_b[:, 0].rearrange("p n b -> p (n b)").bitcast(BF16)[:, 0:P].rearrange("p (n e) -> p n e", e=E)
            mask = rt[2]
            dve.wait_ge(S["x2_ready"], TJ * B + 1)
            V.tensor_tensor(mask16, oh[0], oh[1], ALU.add).then_inc(S["mask_ready"], 1)
            link(V.tensor_tensor(mask.rearrange("p e n -> p n e"), oh[0], oh[1], ALU.add))
            dve.wait_ge(S["exp_ready"], 1)
            link(V.tensor_scalar(den, prob2, 1.0, None, ALU.add))
            link(V.reciprocal(prob1, den))
            dve.wait_ge(S["tanh_ready"], 1)
            link(V.tensor_tensor(prob2, prob2, prob1, ALU.mult))
            link(V.tensor_scalar(tm[:, 2:4, 0:NT], tm[:, 2:4, 0:NT], tanh_g[:, 1:2], None, ALU.mult))
            V.tensor_tensor(oh[0], oh[0], cols(prob1, E), ALU.mult)
            link(V.tensor_tensor(oh[1], oh[1], cols(prob2, E), ALU.mult))
            V.tensor_tensor(top[:], oh[0], oh[1], ALU.add).then_inc(S["cw_row_ready"], 1)
            dve.wait_ge(S["counts_full"], 1)
            within, total = RB[0][:, 0:P].rearrange("p (e n) -> p e n", e=E), RB[1][:, 0:P]
            tot, run, before, rank, u = rt[3], rt[4], rt[5], rt[6], rt[7]
            fl = lambda ap: ap.rearrange("p e n -> p (e n)")
            link(V.tensor_copy(fl(tot), total))
            link(V.memset(fl(rank), 1.0))
            link(V.tensor_tensor_scan(fl(run), fl(rank), fl(tot), 0.0, ALU.mult, ALU.add))
            link(V.tensor_tensor(fl(before), fl(run), fl(tot), ALU.subtract))
            link(V.tensor_tensor(n_e[:, 0, :], run[:, :, NT - 1], before[:, :, 0], ALU.subtract))
            link(V.tensor_tensor(rank, before, before[:, :, 0:1].to_broadcast([P, E, NT]), ALU.subtract))
            link(V.tensor_tensor(rank, within, rank, ALU.add))
            tid = tidx[:].unsqueeze(1).to_broadcast([P, E, NT])
            link(V.tensor_tensor(u, tid, rank, ALU.subtract))
            link(V.tensor_tensor(u, u, cols(n_e[:, 0, :], NT), ALU.add))
            link(V.tensor_tensor(rank, rank, u, ALU.subtract))
            link(V.tensor_tensor(rank, rank, mask, ALU.mult))
            link(V.tensor_tensor(u, u, rank, ALU.add))
            place_i, hi_i, lo_i = rt[8].bitcast(I32), rt[9].bitcast(I32), rt[10].bitcast(I32)
            link(V.tensor_copy(place_i, u))
            V.tensor_scalar(hi_i, place_i, 7, None, ALU.arith_shift_right)
            link(V.tensor_scalar(lo_i, place_i, P - 1, None, ALU.bitwise_and))
            hi, lo = rt[11], rt[12]
            V.tensor_copy(hi, hi_i)
            link(V.tensor_copy(lo, lo_i))
            for e in range(E):
                last = V.tensor_tensor(onehot_a[:, e], iota_a[:].unsqueeze(1).to_broadcast([P, NT, 16]),
                                       cols(hi[:, e, :], 16), ALU.is_equal)
            link(last)
            for e in range(E):
                last = V.tensor_tensor(onehot_a[:, e], onehot_a[:, e], cols(tidx[:], 16), ALU.mult)
            for e in range(E):
                if e >= 2:
                    dve.wait_ge(S["onehot_used"], e - 1)
                V.tensor_tensor(onehot_b[:, e % 2], iota_b[:].unsqueeze(1).to_broadcast([P, NT, P]),
                                cols(lo[:, e, :], P), ALU.is_equal).then_inc(S["onehot_ready"], 1)
            tiles_e, tiles_run = n_e[:, 1, :], n_e[:, 2, :]
            link(V.tensor_scalar(n_e[:, 1, :], n_e[:, 0, :], float(P - 1), None, ALU.add))
            link(V.tensor_copy(n_i[:, 0, :], n_e[:, 1, :]))
            link(V.tensor_scalar(n_i[:, 1, :], n_i[:, 0, :], 7, None, ALU.arith_shift_right))
            link(V.tensor_copy(tiles_e, n_i[:, 1, :]))
            link(V.memset(n_e[:, 3, :], 1.0))
            link(V.tensor_tensor_scan(tiles_run, n_e[:, 3, :], tiles_e, 0.0, ALU.mult, ALU.add))
            iota_s = iota_b[:, 0:IDX_COLS]
            passed = slot_onehot[:]
            link(V.tensor_tensor(passed, cols(iota_s, E), tiles_run.unsqueeze(1).to_broadcast([P, IDX_COLS, E]), ALU.is_ge))
            expert_of, first_of, column, fits = (tm[:, k, :] for k in range(4))
            link(V.tensor_reduce(expert_of, passed, axis=AX.X, op=ALU.add))
            link(V.tensor_tensor(passed, passed, tiles_e.unsqueeze(1).to_broadcast([P, IDX_COLS, E]), ALU.mult))
            link(V.tensor_reduce(first_of, passed, axis=AX.X, op=ALU.add))
            V.tensor_scalar(column, expert_of, float(16), None, ALU.mult)
            link(V.tensor_scalar(fits, expert_of, E - 0.5, None, ALU.is_le))
            link(V.tensor_tensor(column, column, first_of, ALU.subtract))
            link(V.tensor_tensor(column, column, fits, ALU.mult))
            link(V.tensor_tensor(column, column, iota_s, ALU.add))
            V.tensor_scalar(slot_expert[:], expert_of, float(E - 1), None, ALU.min)
            V.tensor_tensor(slot_onehot[:], iota_e[:].unsqueeze(1).to_broadcast([P, IDX_COLS, E]),
                            cols(expert_of, E), ALU.is_equal)
            pick = tm[:, 4, :]
            link(V.tensor_scalar(pick, column, iota_p[:, 0:1], None, ALU.is_equal))
            table, tableT = fl(rt[0]), fl(rt[1])
            dve.wait_ge(S["onehot_used"], E)
            V.tensor_copy(table, RB[0][:, 0:P]).then_inc(S["table_sb"], 1)
            dve.wait_ge(S["tableT_full"], 1)
            V.tensor_copy(tableT, RB[1][:, 0:P]).then_inc(S["tableT_sb"], 1)
            dve.wait_ge(S["slots_full"], 1)
            V.tensor_copy(slot_token[:], AC[0][:, 0:IDX_COLS]).then_inc(S["slots_ready"], 1)
            dve.wait_ge(S["slots_ready"], 1)

            def weight_of(at):
                dve.wait_ge(S["gathered"], at * 16 + 16)
                V.tensor_tensor(cwm, G[:, D:ROW], slot_onehot[:, bass.ds(at, 1), :].rearrange("p a e -> p (a e)"),
                                ALU.mult).then_inc(S["gather_used"], 1)

            def products(at):
                dve.wait_ge(S["h1_full"], at + 1)
                dve.wait_ge(S["sil_ready"], at + 1)
                V.tensor_tensor(HH.rearrange("p c s -> p (c s)"), SIL, AC[1][:], ALU.mult).then_inc(S["hh_ready"], 1)

            def finish(n):
                dve.wait_ge(S["y_full"], n)
                dve.wait_ge(S["ys_free"], n)
                V.tensor_scalar(YS, TV[0][:], cw_tile, None, ALU.mult).then_inc(S["ys_ready"], 1)

            def reduce_weight(at):
                dve.wait_ge(S["gather_used"], at + 1)
                V.tensor_reduce(cw_tile, cwm, axis=AX.X, op=ALU.add).then_inc(S["cw_ready"], 1)

            weight_of(0)
            reduce_weight(0)
            products(0)
            dve.wait_ge(S["cw_ready"], 1)
            with dve.Fori(1, SLOT_TILES) as i:
                weight_of(i)
                products(i)
                finish(i)
                dve.wait_ge(S["ys_ready"], i)
                reduce_weight(i)
                dve.wait_ge(S["cw_ready"], i + 1)
            finish(SLOT_TILES)

        @block.scalar
        def _(act):
            A_ = nc.scalar
            act.sem_inc(S["ta_free"], 2)
            act.wait_ge(S["gates_in"], 32)
            A_.activation(tanh_g[:], gates[:], ACT.Tanh).then_inc(S["tanh_ready"], 1)
            act.wait_ge(S["tanh_ready"], 1)
            with act.Fori(0, B) as b:
                def evacuate(k, dst, bias, ready):
                    act.wait_ge(S["ta_full"], b * 16 + k + 1)
                    A_.activation(dst, TA[k % 2][:], ACT.Copy, bias=bias).then_inc(ready, 1)

                act.wait_ge(S["var_ready"], b + 1)
                A_.activation(sd[:], var_eps[:], ACT.Sqrt).then_inc(S["sd_ready"], 1)
                act.wait_ge(S["ratio_ready"], b * 2 + 1)
                A_.activation(smooth[:, 0, :], ratio[:], ACT.Sqrt).then_inc(S["smooth_sqrt"], 1)
                act.wait_ge(S["qscale_ready"], b * 2 + 1)
                for k in range(8):
                    A_.activation(TQ[:, k, :], TQ[:, k, :], ACT.Copy, bias=MAGIC,
                                  scale=qinv[:, k:k + 1]).then_inc(S["magic_ready"], 1)
                for c in range(DC):
                    evacuate(c, w1qT[:, c, :], -MAGIC, S["ta_free"])
                for c in range(DC):
                    evacuate(DC + c, xqT[:, c, :], -MAGIC, S["ta_free"])
                act.wait_ge(S["ta_free"], b * 16 + 2 + 8)
                A_.sem_inc(S["qT_ready"], 1)
                act.wait_ge(S["scale_row_full"], b * 2 + 1)
                A_.activation(w1_scale_row, RB[0][:], ACT.Copy).then_inc(S["scale_row_ready"], 1)
                for j in range(TJ):
                    act.wait_ge(S["h_ready"], b * 4 + j + 1)
                    A_.activation(TQ[:, 4 + j, 0:I], TQ[:, j, 0:I], ACT.Silu).then_inc(S["silu_ready"], 1)
                act.wait_ge(S["ratio_ready"], b * 2 + 2)
                A_.activation(smooth[:, 0, :], ratio[:], ACT.Sqrt).then_inc(S["smooth_sqrt"], 1)
                act.wait_ge(S["qscale_ready"], b * 2 + 2)
                for k in range(8):
                    A_.activation(TQ2[:, k, :], TQ2[:, k, :], ACT.Copy, bias=MAGIC,
                                  scale=qinv[:, k:k + 1]).then_inc(S["magic2_ready"], 1)
                for c in range(IC):
                    evacuate(8 + c, w2qT[:, c, :], -MAGIC, S["ta_free"])
                for c in range(IC):
                    evacuate(10 + c, aqT[:, c, :], -MAGIC, S["ta_free"])
                act.wait_ge(S["ta_free"], b * 16 + 2 + 12)
                A_.sem_inc(S["qT2_ready"], 1)
                act.wait_ge(S["scale_row_full"], b * 2 + 2)
                A_.activation(w2_scale_row, RB[0][:], ACT.Copy,
                              scale=tanh_g[:, 0:1]).then_inc(S["scale_row_ready"], 1)
                act.wait_ge(S["var2_ready"], b + 1)
                A_.activation(sd[:], var_eps[:], ACT.Sqrt).then_inc(S["sd2_ready"], 1)
                for j in range(TJ):
                    evacuate(12 + j, xn2T[:, j % 2].rearrange("p c t -> p (c t)"), 0.0, S["ta_free"])
            act.wait_ge(S["x2_ready"], TJ * B + 1)
            A_.activation(tm[:, 3, 0:NT], tm[:, 1, 0:NT], ACT.Exp).then_inc(S["exp_ready"], 1)

            def xT(at):
                act.wait_ge(S["xT_full"], at + 1)
                A_.activation(XT.rearrange("p c s -> p (c s)"), TA[0][:], ACT.Copy).then_inc(S["xT_ready"], 1)

            def silu(at):
                act.wait_ge(S["h0_full"], at + 1)
                A_.activation(SIL, AC[0][:], ACT.Silu).then_inc(S["sil_ready"], 1)

            def hT(at):
                act.wait_ge(S["hT_full"], at + 1)
                A_.activation(HT.rearrange("p c s -> p (c s)"), TA[1][:], ACT.Copy).then_inc(S["hT_ready"], 1)

            act.wait_ge(S["slots_ready"], 1)
            xT(0)
            silu(0)
            act.wait_ge(S["h1_full"], 1)
            xT(1)
            with act.Fori(1, SLOT_TILES) as i:
                act.wait_ge(S["hT_full"], i)
                A_.activation(HT.rearrange("p c s -> p (c s)"), TA[1][:], ACT.Copy).then_inc(S["hT_ready"], 1)
                act.wait_ge(S["hh_ready"], i)
                silu(i)
                act.wait_ge(S["h1_full"], i + 1)
                act.wait_ge(S["xT_full"], i + 2)
                A_.activation(XT.rearrange("p c s -> p (c s)"), TA[0][:], ACT.Copy).then_inc(S["xT_ready"], 1)
            hT(SLOT_TILES - 1)

        @block.tensor
        def _(pe):
            T_ = nc.tensor
            pe.wait_ge(S["consts_ready"], 1)
            pe.wait_ge(S["gate_in"], 16)
            with pe.Fori(0, B) as b:
                def turn(k, bank, full, free, per_row, tiles):
                    pe.wait_ge(free, b * per_row + k + 1)
                    for n, t in enumerate(tiles):
                        last = T_.transpose(bank[k % 2][:, n * P:(n + 1) * P], t, ident[:])
                    last.then_inc(full, 1)

                def to_vector(k, tiles):
                    turn(k, TV, S["tv_full"], S["tv_free"], 12, tiles)

                def to_scalar(k, tiles):
                    turn(k, TA, S["ta_full"], S["ta_free"], 16, tiles)

                def spread(bank, col, n):
                    for c in range(n):
                        last = T_.matmul(bank[:, c * P:(c + 1) * P], col[:, c:c + 1].to_broadcast([P, P]),
                                         ident[:], start=True, stop=True)
                    return last

                pe.wait_ge(S["w1_in"], b * 16 + 16)
                for c in range(DC):
                    to_vector(c, [W1[:, r, c * P:(c + 1) * P] for r in range(TJ)])
                pe.wait_ge(S["xn_ready"], b * 4 + 4)
                for c in range(DC):
                    to_vector(DC + c, [XN[:, j, c * P:(c + 1) * P] for j in range(TJ)])
                pe.wait_ge(S["smooth_ready"], b * 2 + 1)
                spread(RB[0], smooth[:, 0, :], DC).then_inc(S["rows_ready"], 1)
                spread(RB[1], smooth[:, 1, :], DC).then_inc(S["rows_ready"], 1)
                pe.wait_ge(S["clip_ready"], b * 8 + 4)
                for c in range(DC):
                    to_scalar(c, [TQ[:, r, c * P:(c + 1) * P] for r in range(TJ)])
                pe.wait_ge(S["clip_ready"], b * 8 + 8)
                for c in range(DC):
                    to_scalar(DC + c, [TQ[:, 4 + j, c * P:(c + 1) * P] for j in range(TJ)])
                spread(RB[0], qscale[:, 0, 0:4], TJ).then_inc(S["scale_row_full"], 1)
                pe.wait_ge(S["qT_ready"], b + 1)
                for j in range(TJ):
                    pe.wait_ge(S["ac_free"], b * 12 + j + 1)
                    for c in range(DC):
                        last = T_.matmul(AC[j % 2][:], xqT[:, c, j * P:(j + 1) * P], w1qT[:, c, :],
                                         start=(c == 0), stop=(c == DC - 1))
                    last.then_inc(S["ac_full"], 1)
                pe.wait_ge(S["w2_in"], b * 16 + 16)
                for c in range(IC):
                    to_vector(8 + c, [W2[:, r, c * P:(c + 1) * P] for r in range(TJ)])
                pe.wait_ge(S["a_ready"], b * 4 + 4)
                for c in range(IC):
                    to_vector(10 + c, [A[:, j, c * P:(c + 1) * P] for j in range(TJ)])
                pe.wait_ge(S["smooth_ready"], b * 2 + 2)
                spread(RB[0], smooth[:, 0, :], IC).then_inc(S["rows_ready"], 1)
                spread(RB[1], smooth[:, 1, :], IC).then_inc(S["rows_ready"], 1)
                pe.wait_ge(S["clip2_ready"], b * 8 + 4)
                for c in range(IC):
                    to_scalar(8 + c, [TQ2[:, r, c * P:(c + 1) * P] for r in range(TJ)])
                pe.wait_ge(S["clip2_ready"], b * 8 + 8)
                for c in range(IC):
                    to_scalar(10 + c, [TQ2[:, 4 + j, c * P:(c + 1) * P] for j in range(TJ)])
                spread(RB[0], qscale[:, 1, 0:4], TJ).then_inc(S["scale_row_full"], 1)
                pe.wait_ge(S["qT2_ready"], b + 1)
                for j in range(TJ):
                    pe.wait_ge(S["ac_free"], b * 12 + 4 + j + 1)
                    for c in range(IC):
                        last = T_.matmul(AC[j % 2][:], aqT[:, c, j * P:(j + 1) * P], w2qT[:, c, :],
                                         start=(c == 0), stop=(c == IC - 1))
                    last.then_inc(S["ac_full"], 1)
                for j in range(TJ):
                    pe.wait_ge(S["xn2_ready"], b * 4 + j + 1)
                    to_scalar(12 + j, [XN[:, j, c * P:(c + 1) * P] for c in range(DC)])
                    pe.wait_ge(S["ta_free"], b * 16 + 12 + j + 1 + 2)
                    pe.wait_ge(S["ac_free"], b * 12 + 8 + j + 1)
                    for c in range(DC):
                        last = T_.matmul(AC[j % 2][:, 0:E], xn2T[:, j % 2, c, :], gate_sb[:, c, :],
                                         start=(c == 0), stop=(c == DC - 1))
                    last.then_inc(S["ac_full"], 1)

            pe.wait_ge(S["mask_ready"], 1)
            mask16 = onehot_b[:, 0].rearrange("p n b -> p (n b)").bitcast(BF16)[:, 0:P].rearrange("p (n e) -> p e n", e=E)
            T_.matmul(RB[0][:, 0:P], upper[:], mask16, start=True, stop=True)
            T_.matmul(RB[1][:, 0:P], ones[:], mask16, start=True, stop=True).then_inc(S["counts_full"], 1)
            for e in range(E):
                pe.wait_ge(S["onehot_ready"], e + 1)
                for n in range(NT):
                    last = T_.matmul(RB[0][:, e * 16:(e + 1) * 16], onehot_b[:, e % 2, n, :], onehot_a[:, e, n, :],
                                     start=(n == 0), stop=(n == NT - 1))
                last.then_inc(S["onehot_used"], 1)
            pe.wait_ge(S["table_sb"], 1)
            T_.transpose(RB[1][:, 0:P], rt[0].rearrange("p e n -> p (e n)"), ident[:]).then_inc(S["tableT_full"], 1)
            pe.wait_ge(S["tableT_sb"], 1)
            T_.matmul(AC[0][:, 0:IDX_COLS], rt[1].rearrange("p e n -> p (e n)"), tm[:, 4, :],
                      start=True, stop=True).then_inc(S["slots_full"], 1)

            def transpose_x(at):
                pe.wait_ge(S["gathered"], at * 16 + 16)
                for c in range(DC):
                    last = T_.transpose(TA[0][:, c * P:(c + 1) * P], G[:, c * P:(c + 1) * P], ident[:])
                last.then_inc(S["xT_full"], 1)

            def up(bank, which, expert, full):
                for c in range(DC):
                    w = experts[:, bass.ds(expert, 1), which * DC + c, :].rearrange("p a n -> p (a n)")
                    last = T_.matmul(bank[:], XT[:, c, :], w, start=(c == 0), stop=(c == DC - 1))
                last.then_inc(full, 1)

            def transpose_h():
                for c in range(MC):
                    last = T_.transpose(TA[1][:, c * P:(c + 1) * P], HH[:, c, :], ident[:])
                last.then_inc(S["hT_full"], 1)

            def down(expert):
                for c in range(MC):
                    w = experts[:, bass.ds(expert, 1), 2 * DC + c, :].rearrange("p a n -> p (a n)")
                    last = T_.matmul(TV[0][:], HT[:, c, :], w, start=(c == 0), stop=(c == MC - 1))
                last.then_inc(S["y_full"], 1)

            pe.wait_ge(S["slots_ready"], 1)
            first = pe.value_load(slot_expert[0:1, 0:1], min_val=0, max_val=E - 1)
            transpose_x(0)
            pe.wait_ge(S["experts_in"], 16 * 3 * E)
            pe.wait_ge(S["xT_ready"], 1)
            up(AC[0], 0, first, S["h0_full"])
            up(AC[1], 1, first, S["h1_full"])
            transpose_x(1)
            with pe.Fori(1, SLOT_TILES) as i:
                expert = pe.value_load(slot_expert[0:1, bass.ds(i, 1)], min_val=0, max_val=E - 1)
                before = pe.value_load(slot_expert[0:1, bass.ds(i - 1, 1)], min_val=0, max_val=E - 1)
                pe.wait_ge(S["xT_ready"], i + 1)
                pe.wait_ge(S["sil_ready"], i)
                up(AC[0], 0, expert, S["h0_full"])
                pe.wait_ge(S["hh_ready"], i)
                transpose_h()
                up(AC[1], 1, expert, S["h1_full"])
                pe.wait_ge(S["gathered"], i * 16 + 32)
                transpose_x(i + 1)
                pe.wait_ge(S["hT_ready"], i)
                pe.wait_ge(S["cw_ready"], i)
                down(before)
            last_expert = pe.value_load(slot_expert[0:1, SLOT_TILES - 1:SLOT_TILES], min_val=0, max_val=E - 1)
            pe.wait_ge(S["hh_ready"], SLOT_TILES)
            transpose_h()
            pe.wait_ge(S["hT_ready"], SLOT_TILES)
            pe.wait_ge(S["cw_ready"], SLOT_TILES)
            down(last_expert)

        @block.gpsimd
        def _(pool):
            G_ = nc.gpsimd
            G_.memset(ident[:], 0.0).then_inc(S["ident_zero"], 1)
            G_.memset(upper[:], 1.0).then_inc(S["ident_zero"], 1)
            G_.memset(ones[:], 1.0)
            G_.iota(iota_e[:], pattern=[[1, E]], base=0, channel_multiplier=0, allow_small_or_imprecise_dtypes=True)
            G_.iota(iota_a[:], pattern=[[1, 16]], base=0, channel_multiplier=0, allow_small_or_imprecise_dtypes=True)
            G_.iota(iota_b[:], pattern=[[1, P]], base=0, channel_multiplier=0, allow_small_or_imprecise_dtypes=True)
            G_.iota(iota_p[:], pattern=[[0, 1]], base=0, channel_multiplier=1, allow_small_or_imprecise_dtypes=True)
            G_.iota(tidx[:], pattern=[[P, NT]], base=0, channel_multiplier=1, allow_small_or_imprecise_dtypes=True)
            pool.wait_ge(S["ident_zero"], 2)
            G_.affine_select(out=upper[:], in_=upper[:], compare_op=ALU.is_gt, fill=0.0, base=0,
                             pattern=[[1, P]], channel_multiplier=-1)
            G_.affine_select(out=ident[:], in_=ident[:], compare_op=ALU.not_equal, fill=1.0, base=0,
                             pattern=[[-1, P]], channel_multiplier=1).then_inc(S["consts_ready"], 1)
            with pool.Fori(0, B) as b:
                for j in range(TJ):
                    pool.wait_ge(S["silu_ready"], b * 4 + j + 1)
                    G_.tensor_tensor(A[:, j, :], TQ[:, 4 + j, 0:I], TQ[:, j, I:2 * I],
                                     ALU.mult).then_inc(S["a_ready"], 1)

            def take(dst, at, n):
                G_.tensor_copy(dst[:], slot_token[:, bass.ds(at, 1)]).then_inc(S["p_chain"], 1)
                pool.wait_ge(S["p_chain"], n)
                pool.sem_inc(S["p_passed"], 1)

            def gather():
                G_.indirect_dma_start(out=G, out_offset=None, in_=rows,
                                      in_offset=bass.IndirectOffsetOnAxis(ap=idx_gather[:, 0:1], axis=0),
                                      ).then_inc(S["gathered"], 16)

            def scatter():
                G_.indirect_dma_start(out=out_rows, in_=YS, in_offset=None, compute_op=ALU.add,
                                      out_offset=bass.IndirectOffsetOnAxis(ap=idx_scatter[:, 0:1], axis=0),
                                      ).then_inc(S["scattered"], 16)

            pool.wait_ge(S["slots_ready"], 1)
            pool.wait_ge(S["weights_out_done"], 16)
            pool.wait_ge(S["rows_done"], 16 * B)
            pool.wait_ge(S["x_out_done"], 16 * B)
            take(idx_gather, 0, 1)
            gather()
            pool.wait_ge(S["xT_full"], 1)
            pool.wait_ge(S["gather_used"], 1)
            take(idx_gather, 1, 2)
            gather()
            pool.sem_inc(S["ys_free"], 1)
            with pool.Fori(2, SLOT_TILES + 1) as k:
                pool.wait_ge(S["xT_full"], k)
                pool.wait_ge(S["gather_used"], k)
                take(idx_gather, k, k * 2 - 1)
                gather()
                take(idx_scatter, k - 2, k * 2)
                pool.wait_ge(S["ys_ready"], k - 1)
                pool.sem_inc(S["p_passed"], 1)
                scatter()
                pool.wait_ge(S["scattered"], (k - 1) * 16)
                pool.sem_inc(S["ys_free"], 1)
            take(idx_scatter, SLOT_TILES - 1, SLOT_TILES * 2 + 1)
            pool.wait_ge(S["ys_ready"], SLOT_TILES)
            scatter()
            pool.wait_ge(S["scattered"], SLOT_TILES * 16)
            pool.wait_ge(S["gathered"], (SLOT_TILES + 1) * 16)


_INS = ["x", "fside_BxS2xS2_0", "ctx_1024", "g_xattn", "g_ffn", "L0_ffn_gate_kernel", "L0_ffn_wi_0", "L0_ffn_wi_1", "L0_ffn_wo"]


def kernel(**inputs):
    import numpy as np
    import concourse.bacc as bacc
    from concourse.bass_utils import run_bass_kernel_spmd

    nc = bacc.Bacc("TRN2", target_bir_lowering=False, num_devices=1, dynamic_dma_scratch_size=4096)
    arrays, args = {}, []
    for name in _INS:
        a = np.ascontiguousarray(inputs[name])
        arrays[f"in_{name}"] = a
        args.append(nc.dram_tensor(f"in_{name}", a.shape, mybir.dt.from_np(a.dtype), kind="ExternalInput").ap())
    args.append(nc.dram_tensor("out", (B, T, D), F32, kind="ExternalOutput").ap())
    program(nc, *args)
    return run_bass_kernel_spmd(nc, [arrays], core_ids=[0]).results[0]["out"]
```

```python
import concourse.bass as bass
from concourse import mybir
from concourse.alu_op_type import AluOpType as ALU
from contextlib import ExitStack

F32, BF16, F16 = mybir.dt.float32, mybir.dt.bfloat16, mybir.dt.float16
I32, U32 = mybir.dt.int32, mybir.dt.uint32
ACT = mybir.ActivationFunctionType
AX = mybir.AxisListType

P = 128
B, T, D = 4, 512, 512
I = 256
E, M, TOPK = 8, 512, 2
TJ = T // P
DC, IC, MC = D // P, I // P, M // P
NT = B * TJ
SLOT_TILES = B * T * TOPK // P + E - 1
IDX_COLS = SLOT_TILES + 2
ROW = D + E
EPS_Q, QMAX, EPS_LN = 1e-6, 127.0, 1e-5
MAGIC = 1.5 * 2.0 ** 23
KC = 3 * DC
KW = KC * M
RING = 3
SPLIT_SCALE = 2.0 ** 8
H_TOP = 2.0 ** 12


def program(nc, x, guw, dw, g_xattn, g_ffn, gate_kernel, wi_0, wi_1, wo, out):
    rows = nc.dram_tensor("token_rows", [B * T, ROW], F32, kind="Internal").ap()
    x_v = x.rearrange("b (j p) d -> b p j d", p=P)
    guw_v = guw.rearrange("b (r p) d -> b p r d", p=P)
    dw_v = dw.rearrange("b (r p) i -> b p r i", p=P)
    out_rows = out.rearrange("b t d -> (b t) d")
    out_v = out_rows.rearrange("(n p) d -> p n d", p=P)
    rows_v = rows.rearrange("(n p) c -> p n c", p=P)
    expert_v = [w.rearrange("e (c p) n -> e p c n", p=P) for w in (wi_0, wi_1, wo)]

    ctx = ExitStack()
    with ctx:
        def sb(name, shape, dt):
            return ctx.enter_context(nc.sbuf_tensor(name, shape, dt))

        def pb(name):
            return ctx.enter_context(nc.psum_tensor(name, [P, 512], F32))

        experts = sb("experts", [P, E, KC, 2, M], F16)
        flat = experts[:].rearrange("p e k h n -> p (e k h n)").bitcast(F32)
        LATE = 3
        cursor = [(E - LATE) * KW]

        def early(words):
            at = cursor[0]
            cursor[0] += words
            assert cursor[0] <= E * KW
            return flat[:, at:at + words]

        X1 = early(TJ * D).rearrange("p (j d) -> p j d", d=D)
        W1 = early(TJ * D).rearrange("p (r d) -> p r d", d=D)
        w1qT = early(DC * T // 2).bitcast(BF16).rearrange("p (c o) -> p c o", c=DC)
        xqT = early(DC * T // 2).bitcast(BF16).rearrange("p (c t) -> p c t", c=DC)
        assert cursor[0] == (E - LATE + 1) * KW
        XR = early(TJ * D).rearrange("p (j d) -> p j d", d=D)
        T1 = early(8 * D).rearrange("p (k d) -> p k d", d=D)
        t2_words = early(8 * I)
        T2 = t2_words.rearrange("p (k i) -> p k i", i=I)
        XN2 = t2_words.rearrange("p (j d) -> p j d", d=D)
        A = early(TJ * I).rearrange("p (j i) -> p j i", i=I)
        W2 = early(TJ * I).rearrange("p (r i) -> p r i", i=I)
        w2qT = early(IC * T // 2).bitcast(BF16).rearrange("p (c o) -> p c o", c=IC)
        aqT = early(IC * T // 2).bitcast(BF16).rearrange("p (c t) -> p c t", c=IC)
        early(1024)
        xn2T = flat[:, cursor[0] - 2048:cursor[0]].rearrange("p (c t) -> p c t", c=DC)

        REGION = 3664
        region = sb("region", [P, REGION], F32)

        def part(at, words):
            assert at + words <= REGION
            return region[:, at:at + words]

        s1_row = part(0, D)
        s2_row = part(512, I)
        w1_scale_row = part(768, D)
        w2_scale_row = part(1280, D)
        OT = part(1792, 2 * D).rearrange("p (s d) -> p s d", s=2)
        logits_e = part(2816, T)
        onehot_b = part(0, NT * P).bitcast(F16).rearrange("p (n b) -> p n b", b=P)
        onehot_u = part(0, E * P).bitcast(F16).rearrange("p (n b) -> p n b", b=P)
        onehot_a = part(2048, NT * IDX_COLS).bitcast(F16).rearrange("p (n a) -> p n a", a=IDX_COLS)
        rt = [part(2704 + P * k, P).rearrange("p (e n) -> p e n", e=E) for k in range(7)]
        mask16 = part(3600, P // 2).bitcast(BF16).rearrange("p (n e) -> p n e", e=E)
        slot_work = part(2704 + 3 * P, IDX_COLS * E).rearrange("p (n e) -> p n e", e=E)
        G = part(0, 2 * ROW).rearrange("p (s c) -> p s c", s=2)
        XT = part(1040, 512).bitcast(F16).rearrange("p (h c s) -> p h c s", h=2, c=DC)
        SIL = part(1552, 512)
        HH = part(2064, 512)
        HT = part(2576, 512).bitcast(F16).rearrange("p (h c s) -> p h c s", h=2, c=MC)
        YS = part(3088, 512)
        cwm = part(3600, E)
        cw_tile, hmax, hcap, hinv, cwy = (part(3608 + k, 1) for k in range(5))

        ring = sb("ring", [P, RING, M], F32)
        ident = sb("ident", [P, P], F32)
        upper = sb("upper", [P, P], BF16)
        ones = sb("ones", [P, P], BF16)
        gate_sb = sb("gate_sb", [P, DC, E], F32)
        bst = sb("bst", [P, 2, TJ, 6], F32)
        mv = sb("mv", [P, 2, TJ, 2], F32)
        var_eps = sb("var_eps", [P, 2, TJ], F32)
        sd = sb("sd", [P, 2, TJ], F32)
        rstd = sb("rstd", [P, 2, TJ], F32)
        shift = sb("shift", [P, 2, TJ], F32)
        amax = sb("amax", [P, 2, 2, 4], F32)
        amax_c = sb("amax_c", [P, 2, 2, 4], F32)
        amax_r = sb("amax_r", [P, 2, 4], F32)
        ratio = sb("ratio", [P, 2, 4], F32)
        smooth = sb("smooth", [P, 2, 2, 4], F32)
        rowmax = sb("rowmax", [P, 2, 2, 4], F32)
        qscale = sb("qscale", [P, 2, 2, 4], F32)
        qinv = sb("qinv", [P, 2, 2, 4], F32)
        gates = sb("gates", [P, 2], F32)
        tanh_g = sb("tanh_g", [P, 2], F32)
        logits = sb("logits", [P, TJ, E], F32)
        top = sb("top", [P, NT, 8], F32)
        choice = sb("choice", [P, NT, TOPK], F32)
        row_top = sb("row_top", [P, TJ, 8], F32)
        row_top_i = sb("row_top_i", [P, TJ, 8], U32)
        n_e = sb("n_e", [P, 4, E], F32)
        n_i = sb("n_i", [P, 2, E], I32)
        iota_e = sb("iota_e", [P, E], F32)
        slot_xy = sb("slot_xy", [P, 3, 2 * NT], F32)
        slot_i = sb("slot_i", [P, 3, 2 * NT], I32)
        spare_e = sb("spare_e", [P, E], F32)
        token16 = sb("token16", [P, 2], F16)
        iota_b = sb("iota_b", [P, P], F32)
        iota_p = sb("iota_p", [P, 1], F32)
        tidx = sb("tidx", [P, NT], F32)
        tm = sb("tm", [P, 5, IDX_COLS], F32)
        slot_expert = sb("slot_expert", [P, IDX_COLS], I32)
        slot_token = sb("slot_token", [P, IDX_COLS], I32)
        slot_onehot = sb("slot_onehot", [P, IDX_COLS, E], F32)
        idx_gather = sb("idx_gather", [P, 2], I32)
        idx_scatter = sb("idx_scatter", [P, 1], I32)

        TV = [pb(f"TV{k}") for k in range(2)]
        TA = [pb(f"TA{k}") for k in range(2)]
        RB = [pb(f"RB{k}") for k in range(2)]
        AC = [pb(f"AC{k}") for k in range(2)]

        counts = dict(
            x1_in=(1, 0), w1_in=(1, 0), w2_in=(0, 1), xr_in=(0, 1), x_out_done=(0, 1), rows_done=(0, 1),
            var_ready=(1, 1), sd_ready=(1, 1), norm_ready=(1, 1), xn_ready=(TJ, 0), xn2_ready=(0, TJ),
            tv_full=(2 * DC, 2 * IC), tv_free=(2 * DC, 2 * IC), ta_full=(2 * DC, 2 * IC + TJ),
            ta_free=(2 * DC, 2 * IC + TJ), ac_full=(TJ, TJ), ac_free=(TJ, TJ),
            ratio_ready=(1, 1), smooth_sqrt=(1, 1), smooth_ready=(1, 1),
            s1_row_full=(1, 0), s1_row_ready=(1, 0), inv1_full=(1, 0), rows2_full=(0, 1), s2_row_ready=(0, 1),
            w1_scaled=(TJ, 0), w2_scaled=(0, TJ), qx_ready=(1, 0), qw_ready=(1, 0), qa_ready=(0, 1), qw2_ready=(0, 1),
            magic1_ready=(8, 0), magic2_ready=(0, 8), scale1_full=(1, 0), scale1_ready=(1, 0),
            scale2_full=(0, 1), scale2_ready=(0, 1), h_ready=(TJ, 0), silu_ready=(TJ, 0), a_ready=(TJ, 0),
            logits_full=(0, 1), logits_sb=(0, 1), logits_t_full=(0, 1), x2_ready=(0, TJ), high_ready=(KC, 0), low_ready=(KC, 0),
        )
        names = """ident_zero consts_ready gates_in gate_in experts_split tanh_ready w_out_done v_chain v_passed pe_passed
            exp_ready diff_ready cw_row_ready mask_ready counts_full onehot_ready
            onehot_u_ready spare_full slots_full slots_ready p_chain p_passed
            weight_taken xT_full xT_high xT_low h0_full h1_full sil_ready hh_ready
            h_scaled hT_full hT_high hT_low y_full ys_ready ys_free cw_ready scattered""".split()
        S = {n: ctx.enter_context(nc.semaphore(n)) for n in list(counts) + names}
        gathered = [ctx.enter_context(nc.semaphore(f"gathered{s}")) for s in range(2)]
        chunk_in = [ctx.enter_context(nc.semaphore(f"chunk_in{k}")) for k in range(RING)]
        block = ctx.enter_context(nc.Block())

        DMA_UNIT = {n: 16 for n in ("x1_in", "w1_in", "w2_in", "xr_in", "x_out_done", "rows_done")}

        class Values:

            def __init__(self):
                self.step, self.past = None, 0

            def enter(self, step, past):
                self.step, self.past = step, past

            def at(self, name, n):
                first, second = counts[name]
                unit = DMA_UNIT.get(name, 1)
                if self.past == 0:
                    return unit * n
                if self.past == B:
                    return unit * (first + (B - 1) * (first + second) + n)
                return self.step * (unit * (first + second)) + unit * (first + n)

        def steps(engine, body, values):
            values.enter(None, 0)
            body(0, None)
            with engine.Fori(0, B - 1) as b:
                values.enter(b, 1)
                body(b + 1, b)
            values.enter(None, B)
            body(None, B - 1)

        def cols(ap, n):
            return ap.unsqueeze(2).to_broadcast([P, ap.shape[1], n])

        expert_chunk = [[expert_v[k // DC][:, :, k % DC, :]] for k in range(KC)]

        @block.sync
        def _(sp):
            def chunk(e, k):
                sp.dma_start(ring[:, k % RING, :],
                             expert_v[k // DC][bass.ds(e, 1), :, k % DC, :].rearrange("a p n -> (a p) n")
                             ).then_inc(chunk_in[k % RING], 16)

            for k in range(RING):
                chunk(0, k)
            for k in range(RING, KC):
                sp.wait_ge(S["low_ready"], k - RING + 1)
                chunk(0, k)
            with sp.Fori(1, E) as e:
                for k in range(KC):
                    sp.wait_ge(S["low_ready"], e * KC + k - RING + 1)
                    chunk(e, k)

        def high_part(act, e, k):
            act.wait_ge(chunk_in[k % RING], e * (16 * KC // RING) + 16 * (k // RING + 1))
            nc.scalar.activation(experts[:, bass.ds(e, 1), k, 0, :].rearrange("p a n -> p (a n)"), ring[:, k % RING, :],
                                 ACT.Copy, scale=SPLIT_SCALE)
            nc.scalar.activation(ring[:, k % RING, :], ring[:, k % RING, :], ACT.Copy,
                                 scale=SPLIT_SCALE).then_inc(S["high_ready"], 1)

        def low_part(pool, e, k):
            pool.wait_ge(S["high_ready"], e * KC + k + 1)
            at = experts[:, bass.ds(e, 1), k, :, :].rearrange("p a h n -> p (a h) n")
            nc.gpsimd.tensor_tensor(at[:, 1, :], ring[:, k % RING, :], at[:, 0, :],
                                    ALU.subtract).then_inc(S["low_ready"], 1)

        def split_turns(emit, engine, e, chunks):
            done = [0]

            def some(n):
                for _ in range(min(n, chunks - done[0])):
                    emit(engine, e + done[0] // KC, done[0] % KC)
                    done[0] += 1
            return some

        def split_share(first, second):
            if second is None:
                return 0, 2 * KC
            return (B + 1, KC) if first is None else (first + 1, KC)

        @block.vector
        def _(dve):
            V = nc.vector
            values = Values()
            chain = [0, 0]
            CHAIN = (12, 16)
            counts["v_chain"] = CHAIN

            def link(ins):
                chain[0] += 1
                ins.then_inc(S["v_chain"], 1)
                dve.wait_ge(S["v_chain"], values.at("v_chain", chain[0]))

            def gap():
                dve.sem_inc(S["v_passed"], 1)

            dve.sem_inc(S["tv_free"], 2)
            dve.sem_inc(S["ac_free"], 2)

            def body(first, second):
                chain[0] = 0
                at = values.at
                two = second is not None
                one = first is not None
                ac = [0]

                def statistics(h, tile_of, name, n):
                    gap()
                    for j in range(TJ):
                        last = V.bn_stats(bst[:, h, j, :], tile_of(j))
                    link(last)
                    gap()
                    for j in range(TJ):
                        last = V.bn_aggr(mv[:, h, j, :], bst[:, h, j, :])
                    link(last)
                    V.tensor_scalar(var_eps[:, h, :], mv[:, h, :, 1], EPS_LN, None,
                                    ALU.add).then_inc(S["var_ready"], 1)

                def normaliser(h, n):
                    dve.wait_ge(S["sd_ready"], at("sd_ready", n))
                    link(V.reciprocal(rstd[:, h, :], sd[:, h, :]))
                    V.scalar_tensor_tensor(shift[:, h, :], mv[:, h, :, 0], -1.0, rstd[:, h, :],
                                           ALU.mult, ALU.mult).then_inc(S["norm_ready"], 1)

                def column_maxima(h, which, k0, n):
                    for c in range(n):
                        dve.wait_ge(S["tv_full"], at("tv_full", k0 + c + 1))
                        last = V.tensor_reduce(amax[:, h, which, c:c + 1], TV[(k0 + c) % 2][:], axis=AX.X,
                                               op=ALU.max, apply_absolute_value=True)
                        last.then_inc(S["tv_free"], 1)

                def smoothing_ratio(h, n, seen):
                    dve.wait_ge(S["tv_free"], 2 + at("tv_free", seen))
                    link(V.tensor_scalar(amax_c[:, h, :, 0:n], amax[:, h, :, 0:n], EPS_Q, None, ALU.max))
                    link(V.reciprocal(amax_r[:, h, 0:n], amax_c[:, h, 0, 0:n]))
                    V.tensor_tensor(ratio[:, h, 0:n], amax_c[:, h, 1, 0:n], amax_r[:, h, 0:n],
                                    ALU.mult).then_inc(S["ratio_ready"], 1)

                def smoothing(h, n, turn):
                    dve.wait_ge(S["smooth_sqrt"], at("smooth_sqrt", turn))
                    link(V.tensor_scalar(smooth[:, h, 0, 0:n], smooth[:, h, 0, 0:n], EPS_Q, None, ALU.max))
                    V.reciprocal(smooth[:, h, 1, 0:n], smooth[:, h, 0, 0:n]).then_inc(S["smooth_ready"], 1)

                def row_scales(h, which, tiles, ready):
                    link(V.tensor_reduce(rowmax[:, h, which, :], tiles, axis=AX.X, op=ALU.max,
                                         apply_absolute_value=True))
                    link(V.tensor_scalar(qscale[:, h, which, :], rowmax[:, h, which, :], EPS_Q, 1.0 / QMAX,
                                         ALU.max, ALU.mult))
                    V.reciprocal(qinv[:, h, which, :], qscale[:, h, which, :]).then_inc(S[ready], 1)

                turn = 1 if two else 0
                tv_second = 2 * IC if two else 0
                if one:
                    dve.wait_ge(S["x1_in"], at("x1_in", 1))
                    statistics(0, lambda j: X1[:, j, :], "var_ready", 1)
                if two:
                    column_maxima(1, 1, 0, IC)
                    column_maxima(1, 0, IC, IC)
                    smoothing_ratio(1, IC, 2 * IC)
                if one:
                    column_maxima(0, 0, tv_second, DC)
                    normaliser(0, 1)
                if two:
                    smoothing(1, IC, 1)
                    dve.wait_ge(S["s2_row_ready"], at("s2_row_ready", 1))
                    for j in range(TJ):
                        last = V.tensor_tensor(T2[:, 4 + j, :], A[:, j, :], RB[1][:, I:2 * I], ALU.mult)
                    link(last)
                    row_scales(1, 1, T2[:, 4:8, :], "qa_ready")
                if one:
                    column_maxima(0, 1, tv_second + DC, DC)
                    smoothing_ratio(0, DC, tv_second + 2 * DC)
                if two:
                    dve.wait_ge(S["w2_scaled"], at("w2_scaled", TJ))
                    row_scales(1, 0, T2[:, 0:4, :], "qw2_ready")
                if one:
                    smoothing(0, DC, turn + 1)
                    dve.wait_ge(S["inv1_full"], at("inv1_full", 1))
                    for j in range(TJ):
                        last = V.tensor_tensor(T1[:, 4 + j, :], X1[:, j, :], RB[0][:], ALU.mult)
                    link(last)
                    row_scales(0, 1, T1[:, 4:8, :], "qx_ready")
                if two:
                    dve.wait_ge(S["scale2_ready"], at("scale2_ready", 1))
                    for j in range(TJ):
                        dve.wait_ge(S["ac_full"], at("ac_full", ac[0] + 1))
                        if j >= 2:
                            dve.wait_ge(S["x2_ready"], at("x2_ready", j - 1))
                        V.scalar_tensor_tensor(OT[:, j % 2, :], AC[j % 2][:], qscale[:, 1, 1, j:j + 1],
                                               w2_scale_row, ALU.mult, ALU.mult).then_inc(S["ac_free"], 1)
                        ac[0] += 1
                if one:
                    dve.wait_ge(S["w1_scaled"], at("w1_scaled", TJ))
                    row_scales(0, 0, T1[:, 0:4, :], "qw_ready")
                if two:
                    dve.wait_ge(S["x2_ready"], at("x2_ready", TJ))
                    statistics(1, lambda j: XR[:, j, :], "var_ready", turn + 1)
                if one:
                    dve.wait_ge(S["scale1_ready"], at("scale1_ready", 1))
                    for j in range(TJ):
                        dve.wait_ge(S["ac_full"], at("ac_full", ac[0] + 1))
                        V.scalar_tensor_tensor(T1[:, j, :], AC[j % 2][:], qscale[:, 0, 1, j:j + 1],
                                               w1_scale_row, ALU.mult, ALU.mult).then_inc(S["ac_free"], 1)
                        ac[0] += 1
                if two:
                    normaliser(1, 2 if one else 1)
                if two:
                    dve.wait_ge(S["logits_t_full"], at("logits_t_full", 1))
                    link(V.tensor_copy(logits[:].rearrange("p j e -> p (j e)"), AC[1][:, 0:TJ * E]))
                    gap()
                    for j in range(TJ):
                        last = V.max(row_top[:, j, :], logits[:, j, :])
                    link(last)
                    gap()
                    for j in range(TJ):
                        last = V.max_index(row_top_i[:, j, :], row_top[:, j, :], logits[:, j, :])
                    link(last)
                    V.tensor_copy(top[:, bass.ds(second * TJ, TJ), :], row_top[:])
                    link(V.tensor_copy(choice[:, bass.ds(second * TJ, TJ), :], row_top_i[:, :, 0:2]))
                want = (CHAIN[0] if one else 0) + (CHAIN[1] if two else 0)
                assert chain[0] <= want, chain[0]
                if chain[0] < want:
                    dve.sem_inc(S["v_chain"], want - chain[0])

            dve.wait_ge(S["consts_ready"], 1)
            steps(dve, body, values)
            dve.wait_ge(S["ac_free"], 2 + TJ * 2 * B)
            base = sum(CHAIN) * B
            chain[0] = 0

            def link(ins):
                chain[0] += 1
                ins.then_inc(S["v_chain"], 1)
                dve.wait_ge(S["v_chain"], base + chain[0])

            oh = [rt[k].rearrange("p e n -> p (e n)").rearrange("p (n e) -> p n e", e=E) for k in range(2)]
            diff, prob1, prob2, den = (tm[:, k, 0:NT] for k in (1, 2, 3, 4))
            iota_ne = iota_e[:].unsqueeze(1).to_broadcast([P, NT, E])
            V.tensor_tensor(diff, top[:, :, 1], top[:, :, 0], ALU.subtract).then_inc(S["diff_ready"], 1)
            V.tensor_tensor(oh[0], iota_ne, choice[:, :, 0:1].to_broadcast([P, NT, E]), ALU.is_equal)
            link(V.tensor_tensor(oh[1], iota_ne, choice[:, :, 1:2].to_broadcast([P, NT, E]), ALU.is_equal))
            V.tensor_tensor(mask16, oh[0], oh[1], ALU.add).then_inc(S["mask_ready"], 1)
            dve.wait_ge(S["mask_ready"], 1)
            fl = lambda ap: ap.rearrange("p e n -> p (e n)")
            dve.wait_ge(S["counts_full"], 1)
            within, total = RB[0][:, 0:P].rearrange("p (e n) -> p e n", e=E), RB[1][:, 0:P]
            tot, run, before, rank = rt[3], rt[4], rt[5], rt[6]
            V.tensor_copy(fl(tot), total)
            link(V.memset(fl(rank), 1.0))
            link(V.tensor_tensor_scan(fl(run), fl(rank), fl(tot), 0.0, ALU.mult, ALU.add))
            link(V.tensor_tensor(fl(before), fl(run), fl(tot), ALU.subtract))
            V.tensor_tensor(n_e[:, 0, :], run[:, :, NT - 1], before[:, :, 0], ALU.subtract)
            link(V.tensor_tensor(rank, before, before[:, :, 0:1].to_broadcast([P, E, NT]), ALU.subtract))
            link(V.tensor_tensor(rank, within, rank, ALU.add))
            aside = slot_work[:, 0:2 * E, 0].rearrange("p (e n) -> p e n", n=2)
            link(V.tensor_tensor(aside, tidx[:, 0:2].unsqueeze(1).to_broadcast([P, E, 2]), rank[:, :, 0:2], ALU.subtract))
            link(V.scalar_tensor_tensor(aside, mask16[:, 0:2, :].rearrange("p n e -> p e n"), float(B * T), aside,
                                        ALU.mult, ALU.add))
            V.tensor_tensor(onehot_u, iota_b[:].unsqueeze(1).to_broadcast([P, 2 * E, P]),
                            cols(aside.rearrange("p e n -> p (e n)"), P), ALU.is_equal).then_inc(S["onehot_u_ready"], 1)
            tiles_e, tiles_run = n_e[:, 1, :], n_e[:, 2, :]
            link(V.tensor_scalar(n_e[:, 1, :], n_e[:, 0, :], float(P - 1), None, ALU.add))
            V.memset(n_e[:, 3, :], 1.0)
            link(V.tensor_copy(n_i[:, 0, :], n_e[:, 1, :]))
            link(V.tensor_scalar(n_i[:, 1, :], n_i[:, 0, :], 7, None, ALU.arith_shift_right))
            link(V.tensor_copy(tiles_e, n_i[:, 1, :]))
            link(V.tensor_tensor_scan(tiles_run, n_e[:, 3, :], tiles_e, 0.0, ALU.mult, ALU.add))
            link(V.tensor_tensor(n_e[:, 3, :], tiles_run, tiles_e, ALU.subtract))
            link(V.scalar_tensor_tensor(rank, cols(n_e[:, 3, :], NT), float(P), rank, ALU.mult, ALU.add))
            for k in range(2):
                last = V.tensor_tensor(rt[3 + k].rearrange("p e n -> p (e n)").rearrange("p (n e) -> p n e", e=E), oh[k],
                                rank.rearrange("p e n -> p n e"), ALU.mult)
            link(last)
            slot_kn = slot_xy[:, 0, :]
            for k in range(2):
                last = V.tensor_reduce(slot_xy[:, 0, k * NT:(k + 1) * NT],
                                       rt[3 + k].rearrange("p e n -> p (e n)").rearrange("p (n e) -> p n e", e=E),
                                       axis=AX.X, op=ALU.add)
            link(last)
            link(V.tensor_copy(slot_i[:, 0, :], slot_kn))
            V.tensor_scalar(slot_i[:, 1, :], slot_i[:, 0, :], 7, None, ALU.arith_shift_right)
            link(V.tensor_scalar(slot_i[:, 2, :], slot_i[:, 0, :], P - 1, None, ALU.bitwise_and))
            link(V.tensor_copy(slot_xy[:, 1:3, :], slot_i[:, 1:3, :]))
            link(V.tensor_tensor(onehot_a, iota_b[:, 0:IDX_COLS].unsqueeze(1).to_broadcast([P, 2 * NT, IDX_COLS]),
                                 cols(slot_xy[:, 1, :], IDX_COLS), ALU.is_equal))
            for k in range(2):
                V.tensor_tensor(onehot_a[:, k * NT:(k + 1) * NT], onehot_a[:, k * NT:(k + 1) * NT],
                                cols(tidx[:], IDX_COLS), ALU.mult)
            dve.wait_ge(S["spare_full"], 1)
            for t in range(4):
                at = slice(t * 8, t * 8 + 8)
                V.tensor_tensor(onehot_b[:, at], iota_b[:].unsqueeze(1).to_broadcast([P, 8, P]),
                                cols(slot_xy[:, 2, at], P), ALU.is_equal).then_inc(S["onehot_ready"], 1)
            dve.wait_ge(S["exp_ready"], 1)
            link(V.tensor_scalar(den, prob2, 1.0, None, ALU.add))
            link(V.reciprocal(prob1, den))
            link(V.tensor_tensor(prob2, prob2, prob1, ALU.mult))
            link(V.tensor_scalar(tm[:, 2:4, 0:NT], tm[:, 2:4, 0:NT], tanh_g[:, 1:2], None, ALU.mult))
            V.tensor_tensor(oh[0], oh[0], cols(prob1, E), ALU.mult)
            link(V.tensor_tensor(oh[1], oh[1], cols(prob2, E), ALU.mult))
            V.tensor_tensor(top[:], oh[0], oh[1], ALU.add).then_inc(S["cw_row_ready"], 1)
            iota_s = iota_b[:, 0:IDX_COLS]
            expert_of, first_of, count_of, pad_of, is_pad = (tm[:, k, :] for k in range(5))
            passed, product = slot_onehot[:], slot_work
            link(V.tensor_tensor(passed, cols(iota_s, E), tiles_run.unsqueeze(1).to_broadcast([P, IDX_COLS, E]), ALU.is_ge))
            V.tensor_reduce(expert_of, passed, axis=AX.X, op=ALU.add)
            link(V.tensor_tensor(product, passed, tiles_e.unsqueeze(1).to_broadcast([P, IDX_COLS, E]), ALU.mult))
            link(V.tensor_reduce(first_of, product, axis=AX.X, op=ALU.add))
            V.tensor_scalar(slot_expert[:], expert_of, float(E - 1), None, ALU.min)
            link(V.tensor_tensor(slot_onehot[:], iota_e[:].unsqueeze(1).to_broadcast([P, IDX_COLS, E]),
                                 cols(expert_of, E), ALU.is_equal))
            link(V.tensor_tensor(product, slot_onehot[:], n_e[:, 0, :].unsqueeze(1).to_broadcast([P, IDX_COLS, E]), ALU.mult))
            link(V.tensor_reduce(count_of, product, axis=AX.X, op=ALU.add))
            few, spare = n_e[:, 3, :], spare_e[:]
            V.tensor_scalar(few, n_e[:, 0, :], float(P), None, ALU.is_lt)
            link(V.tensor_scalar(spare, RB[1][:, P:P + E], iota_p[:, 0:1], None, ALU.subtract))
            link(V.tensor_tensor(spare, spare, few, ALU.mult))
            V.tensor_tensor(first_of, iota_s, first_of, ALU.subtract)
            link(V.tensor_tensor(product, slot_onehot[:], spare.unsqueeze(1).to_broadcast([P, IDX_COLS, E]), ALU.mult))
            V.tensor_reduce(pad_of, product, axis=AX.X, op=ALU.add)
            link(V.tensor_scalar(first_of, first_of, float(P), iota_p[:, 0:1], ALU.mult, ALU.add))
            link(V.tensor_tensor(is_pad, first_of, count_of, ALU.is_ge))
            link(V.tensor_scalar(pad_of, pad_of, iota_p[:, 0:1], None, ALU.add))
            V.tensor_tensor(first_of, first_of, count_of, ALU.is_lt)
            link(V.tensor_tensor(pad_of, pad_of, is_pad, ALU.mult))
            dve.wait_ge(S["slots_full"], 1)
            V.tensor_tensor(slot_token[:], RB[0][:, 0:IDX_COLS], pad_of, ALU.add).then_inc(S["slots_ready"], 1)
            link(V.tensor_tensor(slot_onehot[:], slot_onehot[:], cols(first_of, E), ALU.mult))

            def take_weights(at, s, turn):
                dve.wait_ge(gathered[s], turn * 16)
                V.tensor_tensor(cwm, G[:, s, D:ROW], slot_onehot[:, bass.ds(at, 1), :].rearrange("p a e -> p (a e)"),
                                ALU.mult).then_inc(S["weight_taken"], 1)

            def x_low(at):
                dve.wait_ge(S["xT_high"], at + 1)
                V.scalar_tensor_tensor(XT[:, 1].rearrange("p c s -> p (c s)"), TV[0][:], SPLIT_SCALE,
                                       XT[:, 0].rearrange("p c s -> p (c s)"), ALU.mult,
                                       ALU.subtract).then_inc(S["xT_low"], 1)

            def h_low(at):
                dve.wait_ge(S["hT_high"], at + 1)
                V.scalar_tensor_tensor(HT[:, 1].rearrange("p c s -> p (c s)"), TV[1][:], 1.0,
                                       HT[:, 0].rearrange("p c s -> p (c s)"), ALU.mult,
                                       ALU.subtract).then_inc(S["hT_low"], 1)

            def hidden(at):
                dve.wait_ge(S["sil_ready"], at + 1)
                dve.wait_ge(S["h1_full"], at + 1)
                V.tensor_tensor(HH, SIL, AC[1][:], ALU.mult).then_inc(S["hh_ready"], 1)
                dve.wait_ge(S["hh_ready"], at + 1)
                V.tensor_reduce(hmax, HH, axis=AX.X, op=ALU.max,
                                apply_absolute_value=True).then_inc(S["v_chain"], 1)
                dve.wait_ge(S["v_chain"], v0 + at * 3 + 1)
                V.tensor_scalar(hcap, hmax, 1e-30, 1.0 / H_TOP, ALU.max, ALU.mult).then_inc(S["v_chain"], 1)
                dve.wait_ge(S["v_chain"], v0 + at * 3 + 2)
                V.reciprocal(hinv, hcap).then_inc(S["v_chain"], 1)
                dve.wait_ge(S["v_chain"], v0 + at * 3 + 3)
                V.tensor_scalar(HH, HH, hinv, None, ALU.mult).then_inc(S["h_scaled"], 1)

            def output(n):
                dve.wait_ge(S["y_full"], n)
                dve.wait_ge(S["ys_free"], n)
                V.tensor_scalar(YS, RB[0][:], cwy, None, ALU.mult).then_inc(S["ys_ready"], 1)

            def weights(at):
                V.tensor_reduce(cw_tile, cwm, axis=AX.X, op=ALU.add).then_inc(S["cw_ready"], 1)
                dve.wait_ge(S["cw_ready"], at * 2 + 1)
                V.scalar_tensor_tensor(cwy, cw_tile, SPLIT_SCALE ** -3, hcap, ALU.mult,
                                       ALU.mult).then_inc(S["cw_ready"], 1)

            v0 = base + chain[0]
            take_weights(0, 0, 1)
            x_low(0)
            hidden(0)
            dve.wait_ge(S["weight_taken"], 1)
            weights(0)
            x_low(1)
            with dve.Fori(1, SLOT_TILES // 2 + 1) as pair:
                for s in range(2):
                    i = pair * 2 + (s - 1)
                    h_low(i - 1)
                    take_weights(i, 1 - s, pair + s)
                    dve.wait_ge(S["h1_full"], i + 1)
                    x_low(i + 1)
                    hidden(i)
                    output(i)
                    dve.wait_ge(S["ys_ready"], i)
                    weights(i)
            h_low(SLOT_TILES - 1)
            dve.wait_ge(S["cw_ready"], 2 * SLOT_TILES)
            output(SLOT_TILES)

        @block.scalar
        def _(act):
            C = nc.scalar
            values = Values()

            def load(dst, src, row, sem):
                act.dma_start(dst, src[bass.ds(row, 1)].rearrange("a p j d -> (a p) j d")).then_inc(S[sem], 16)

            load(X1, x_v, 0, "x1_in")
            load(W1, guw_v, 0, "w1_in")
            act.dma_start(gates[:, 0:1], g_xattn.unsqueeze(0).to_broadcast([P, 1])).then_inc(S["gates_in"], 16)
            act.dma_start(gates[:, 1:2], g_ffn.unsqueeze(0).to_broadcast([P, 1])).then_inc(S["gates_in"], 16)
            act.dma_start(gate_sb[:], gate_kernel.rearrange("(c p) e -> p c e", p=P)).then_inc(S["gate_in"], 16)
            load(W2, dw_v, 0, "w2_in")
            load(XR, x_v, 0, "xr_in")
            act.sem_inc(S["ta_free"], 2)
            act.wait_ge(S["gates_in"], 32)
            C.activation(tanh_g[:], gates[:], ACT.Tanh).then_inc(S["tanh_ready"], 1)
            act.wait_ge(S["tanh_ready"], 1)

            def body(first, second):
                at = values.at
                one, two = first is not None, second is not None
                turn = 1 if two else 0
                ta = [0]
                high = split_turns(high_part, act, *split_share(first, second))

                def evacuate(dst, bias):
                    act.wait_ge(S["ta_full"], at("ta_full", ta[0] + 1))
                    bank = TA[ta[0] % 2][:]
                    if len(dst.shape) == 3:
                        bank = bank.rearrange("p (c t) -> p c t", c=dst.shape[1])
                    C.activation(dst, bank, ACT.Copy, bias=bias).then_inc(S["ta_free"], 1)
                    ta[0] += 1

                def deviations(h, n):
                    act.wait_ge(S["var_ready"], at("var_ready", n))
                    C.activation(sd[:, h, :], var_eps[:, h, :], ACT.Sqrt).then_inc(S["sd_ready"], 1)

                def smooth_root(h, n, turn):
                    act.wait_ge(S["ratio_ready"], at("ratio_ready", turn))
                    C.activation(smooth[:, h, 0, 0:n], ratio[:, h, 0:n], ACT.Sqrt).then_inc(S["smooth_sqrt"], 1)

                def normalise(h, n, src, dst, ready):
                    act.wait_ge(S["norm_ready"], at("norm_ready", n))
                    for j in range(TJ):
                        C.activation(dst[:, j, :], src[:, j, :], ACT.Identity, bias=shift[:, h, j:j + 1],
                                     scale=rstd[:, h, j:j + 1]).then_inc(S[ready], 1)

                def round_rows(h, which, tiles, wait, ready):
                    act.wait_ge(S[wait], at(wait, 1))
                    for j in range(TJ):
                        C.activation(tiles[:, j, :], tiles[:, j, :], ACT.Copy, bias=MAGIC,
                                     scale=qinv[:, h, which, j:j + 1]).then_inc(S[ready], 1)

                if one:
                    deviations(0, 1)
                if two:
                    smooth_root(1, IC, 1)
                high(2)
                if one:
                    normalise(0, 1, X1, X1, "xn_ready")
                if two:
                    act.wait_ge(S["rows2_full"], at("rows2_full", 1))
                    C.activation(s2_row, RB[1][:, 0:I], ACT.Copy).then_inc(S["s2_row_ready"], 1)
                    round_rows(1, 1, T2[:, 4:8, :], "qa_ready", "magic2_ready")
                    for c in range(IC):
                        evacuate(aqT[:, c, :], -MAGIC)
                high(3)
                if one:
                    smooth_root(0, DC, turn + 1)
                    act.wait_ge(S["s1_row_full"], at("s1_row_full", 1))
                    C.activation(s1_row, RB[0][:], ACT.Copy).then_inc(S["s1_row_ready"], 1)
                if two:
                    round_rows(1, 0, T2[:, 0:4, :], "qw2_ready", "magic2_ready")
                    load(W2, dw_v, (second + 1) % B, "w2_in")
                    for c in range(IC):
                        evacuate(w2qT[:, c, :], -MAGIC)
                    act.wait_ge(S["scale2_full"], at("scale2_full", 1))
                    C.activation(w2_scale_row, RB[1][:], ACT.Copy,
                                 scale=tanh_g[:, 0:1]).then_inc(S["scale2_ready"], 1)
                high(2)
                if one:
                    round_rows(0, 1, T1[:, 4:8, :], "qx_ready", "magic1_ready")
                    load(X1, x_v, (first + 1) % B, "x1_in")
                    for c in range(DC):
                        evacuate(xqT[:, c, :], -MAGIC)
                high(2)
                if one:
                    round_rows(0, 0, T1[:, 0:4, :], "qw_ready", "magic1_ready")
                    load(W1, guw_v, (first + 1) % B, "w1_in")
                    for c in range(DC):
                        evacuate(w1qT[:, c, :], -MAGIC)
                    act.wait_ge(S["scale1_full"], at("scale1_full", 1))
                    C.activation(w1_scale_row, RB[0][:], ACT.Copy).then_inc(S["scale1_ready"], 1)
                if two:
                    deviations(1, 2 if one else 1)
                    act.dma_start(out_v[:, bass.ds(second * TJ, TJ), :], XR).then_inc(S["x_out_done"], 16)
                    normalise(1, 2 if one else 1, XR, XN2, "xn2_ready")
                if one:
                    for j in range(TJ):
                        act.wait_ge(S["ac_free"], 2 + at("ac_free", (TJ if two else 0) + j + 1))
                        C.activation(T1[:, 4 + j, 0:I], T1[:, j, 0:I], ACT.Silu).then_inc(S["silu_ready"], 1)
                if two:
                    act.wait_ge(S["xn2_ready"], at("xn2_ready", TJ))
                    act.dma_start(rows_v[:, bass.ds(second * TJ, TJ), 0:D], XN2).then_inc(S["rows_done"], 16)
                    for j in range(TJ):
                        evacuate(xn2T[:, :, j * P:(j + 1) * P], 0.0)
                    act.wait_ge(S["logits_full"], at("logits_full", 1))
                    C.activation(logits_e[0:E, :], AC[0][0:E, :], ACT.Copy).then_inc(S["logits_sb"], 1)
                if not one:
                    act.wait_ge(S["x1_in"], 16 * (B + 1))
                    act.wait_ge(S["w1_in"], 16 * (B + 1))
                high(2 * KC)
                if two:
                    act.wait_ge(S["x_out_done"], at("x_out_done", 1))
                    load(XR, x_v, (second + 1) % B, "xr_in")
                    act.wait_ge(S["rows_done"], at("rows_done", 1))

            steps(act, body, values)
            act.wait_ge(S["diff_ready"], 1)
            C.activation(tm[:, 3, 0:NT], tm[:, 1, 0:NT], ACT.Exp).then_inc(S["exp_ready"], 1)
            act.wait_ge(S["ac_free"], 2 + 2 * TJ * B)
            act.wait_ge(S["w2_in"], 16 * (B + 1))
            act.wait_ge(S["xr_in"], 16 * (B + 1))
            high = split_turns(high_part, act, B + 2, 2 * KC)
            high(2 * KC)

            def x_high(at):
                act.wait_ge(S["xT_full"], at + 1)
                C.activation(XT[:, 0].rearrange("p c s -> p (c s)"), TV[0][:], ACT.Copy,
                             scale=SPLIT_SCALE).then_inc(S["xT_high"], 1)

            def silu(at):
                act.wait_ge(S["h0_full"], at + 1)
                C.activation(SIL, AC[0][:], ACT.Silu, scale=SPLIT_SCALE ** -2).then_inc(S["sil_ready"], 1)

            def h_high(at):
                act.wait_ge(S["hT_full"], at + 1)
                C.activation(HT[:, 0].rearrange("p c s -> p (c s)"), TV[1][:], ACT.Copy).then_inc(S["hT_high"], 1)

            act.wait_ge(S["slots_ready"], 1)
            x_high(0)
            silu(0)
            act.wait_ge(S["h1_full"], 1)
            x_high(1)
            with act.Fori(1, SLOT_TILES) as i:
                h_high(i - 1)
                silu(i)
                act.wait_ge(S["h1_full"], i + 1)
                x_high(i + 1)
            h_high(SLOT_TILES - 1)

        @block.tensor
        def _(pe):
            T_ = nc.tensor
            values = Values()
            pe.wait_ge(S["consts_ready"], 1)
            pe.wait_ge(S["gate_in"], 16)

            def body(first, second):
                at = values.at
                one, two = first is not None, second is not None
                tv, ta, ac = [0], [0], [0]

                def transposes(k, banks, full, free, tiles):
                    pe.wait_ge(S[free], 1 + at(free, k[0]))
                    for n, t in enumerate(tiles):
                        last = T_.transpose(banks[k[0] % 2][:, n * P:(n + 1) * P], t, ident[:])
                    last.then_inc(S[full], 1)
                    k[0] += 1

                def to_vector(tiles):
                    transposes(tv, TV, "tv_full", "tv_free", tiles)

                def to_scalar(tiles):
                    transposes(ta, TA, "ta_full", "ta_free", tiles)

                def chunks(tiles, n):
                    return [[tiles[:, j, c * P:(c + 1) * P] for j in range(TJ)] for c in range(n)]

                def spread(bank, at_col, col, n):
                    for c in range(n):
                        last = T_.matmul(bank[:, at_col + c * P:at_col + (c + 1) * P],
                                         col[:, c:c + 1].to_broadcast([P, P]), ident[:], start=True, stop=True)
                    return last

                def product(aT, wT, n):
                    for j in range(TJ):
                        pe.wait_ge(S["ac_free"], 1 + at("ac_free", ac[0]))
                        for c in range(n):
                            last = T_.matmul(AC[j % 2][:], aT[:, c, j * P:(j + 1) * P], wT[:, c, :],
                                             start=(c == 0), stop=(c == n - 1))
                        last.then_inc(S["ac_full"], 1)
                        ac[0] += 1

                if two:
                    pe.wait_ge(S["a_ready"], values.at("a_ready", 0))
                    for tiles in chunks(A, IC):
                        to_vector(tiles)
                    pe.wait_ge(S["w2_in"], at("w2_in", 1))
                    for tiles in chunks(W2, IC):
                        to_vector(tiles)
                if one:
                    pe.wait_ge(S["w1_in"], at("w1_in", 1))
                    for tiles in chunks(W1, DC):
                        to_vector(tiles)
                if two:
                    pe.wait_ge(S["smooth_ready"], at("smooth_ready", 1))
                    spread(RB[1], 0, smooth[:, 1, 0, :], IC)
                    spread(RB[1], I, smooth[:, 1, 1, :], IC).then_inc(S["rows2_full"], 1)
                if one:
                    pe.wait_ge(S["xn_ready"], at("xn_ready", TJ))
                    for tiles in chunks(X1, DC):
                        to_vector(tiles)
                if two:
                    pe.wait_ge(S["magic2_ready"], at("magic2_ready", TJ))
                    for tiles in chunks(T2[:, 4:8, :], IC):
                        to_scalar(tiles)
                if one:
                    pe.wait_ge(S["smooth_ready"], at("smooth_ready", 2 if two else 1))
                    spread(RB[0], 0, smooth[:, 0, 0, :], DC).then_inc(S["s1_row_full"], 1)
                    pe.wait_ge(S["s1_row_ready"], at("s1_row_ready", 1))
                    spread(RB[0], 0, smooth[:, 0, 1, :], DC).then_inc(S["inv1_full"], 1)
                if two:
                    pe.wait_ge(S["magic2_ready"], at("magic2_ready", 8))
                    for tiles in chunks(T2[:, 0:4, :], IC):
                        to_scalar(tiles)
                    spread(RB[1], 0, qscale[:, 1, 0, :], TJ).then_inc(S["scale2_full"], 1)
                    pe.wait_ge(S["ta_free"], 2 + at("ta_free", 2 * IC))
                    product(aqT, w2qT, IC)
                if one:
                    pe.wait_ge(S["magic1_ready"], at("magic1_ready", TJ))
                    for tiles in chunks(T1[:, 4:8, :], DC):
                        to_scalar(tiles)
                    pe.wait_ge(S["magic1_ready"], at("magic1_ready", 8))
                    for tiles in chunks(T1[:, 0:4, :], DC):
                        to_scalar(tiles)
                    spread(RB[0], 0, qscale[:, 0, 0, :], TJ).then_inc(S["scale1_full"], 1)
                    pe.wait_ge(S["ta_free"], 2 + at("ta_free", ta[0]))
                    product(xqT, w1qT, DC)
                if two:
                    for j in range(TJ):
                        pe.wait_ge(S["xn2_ready"], at("xn2_ready", j + 1))
                        to_scalar([XN2[:, j, c * P:(c + 1) * P] for c in range(DC)])
                    pe.wait_ge(S["ta_free"], 2 + at("ta_free", ta[0]))
                    pe.wait_ge(S["ac_free"], 2 + at("ac_free", ac[0]))
                    for c in range(DC):
                        last = T_.matmul(AC[0][0:E, :], gate_sb[:, c, :], xn2T[:, c, :],
                                         start=(c == 0), stop=(c == DC - 1))
                    last.then_inc(S["logits_full"], 1)
                    pe.wait_ge(S["logits_sb"], at("logits_sb", 1))
                    pe.sem_inc(S["pe_passed"], 1)
                    for j in range(TJ):
                        last = T_.transpose(AC[1][:, j * E:(j + 1) * E], logits_e[0:E, j * P:(j + 1) * P],
                                            ident[0:E, 0:E])
                    last.then_inc(S["logits_t_full"], 1)

            steps(pe, body, values)

            pe.wait_ge(S["mask_ready"], 1)
            mask_en = mask16.rearrange("p n e -> p e n")
            T_.matmul(RB[0][:, 0:P], upper[:], mask_en, start=True, stop=True)
            T_.matmul(RB[1][:, 0:P], ones[:], mask_en, start=True, stop=True).then_inc(S["counts_full"], 1)
            pe.wait_ge(S["onehot_u_ready"], 1)
            for e in range(E):
                for n in range(2):
                    last = T_.matmul(RB[1][:, P + e:P + e + 1], onehot_u[:, e * 2 + n, :], token16[:, n:n + 1],
                                     start=(n == 0), stop=(n == 1))
            last.then_inc(S["spare_full"], 1)
            for t in range(4):
                pe.wait_ge(S["onehot_ready"], t + 1)
                for n in range(t * 8, t * 8 + 8):
                    last = T_.matmul(RB[0][:, 0:IDX_COLS], onehot_b[:, n, :], onehot_a[:, n, :],
                                     start=(n == 0), stop=(n == 2 * NT - 1))
            last.then_inc(S["slots_full"], 1)

            def transpose_x(s, turn):
                pe.wait_ge(gathered[s], turn * 16)
                for c in range(DC):
                    last = T_.transpose(TV[0][:, c * P:(c + 1) * P], G[:, s, c * P:(c + 1) * P], ident[:])
                last.then_inc(S["xT_full"], 1)

            def transpose_h():
                for c in range(MC):
                    last = T_.transpose(TV[1][:, c * P:(c + 1) * P], HH[:, c * P:(c + 1) * P], ident[:])
                last.then_inc(S["hT_full"], 1)

            def split_product(bank, act_T, expert, k0, full):
                for c in range(DC):
                    w = experts[:, bass.ds(expert, 1), k0 + c, :, :].rearrange("p a h n -> p (a h) n")
                    for n, (ah, wh) in enumerate(((0, 0), (0, 1), (1, 0))):
                        last = T_.matmul(bank[:], act_T[:, ah, c, :], w[:, wh, :],
                                         start=(c == 0 and n == 0), stop=(c == DC - 1 and n == 2))
                last.then_inc(S[full], 1)

            pe.wait_ge(S["slots_ready"], 1)
            first = pe.value_load(slot_expert[0:1, 0:1], min_val=0, max_val=E - 1)
            transpose_x(0, 1)
            pe.wait_ge(S["low_ready"], KC * E)
            pe.wait_ge(S["xT_low"], 1)
            split_product(AC[0], XT, first, 0, "h0_full")
            split_product(AC[1], XT, first, DC, "h1_full")
            transpose_x(1, 1)
            with pe.Fori(1, SLOT_TILES // 2 + 1) as pair:
                for s in range(2):
                    i = pair * 2 + (s - 1)
                    expert = pe.value_load(slot_expert[0:1, bass.ds(i, 1)], min_val=0, max_val=E - 1)
                    before = pe.value_load(slot_expert[0:1, bass.ds(i - 1, 1)], min_val=0, max_val=E - 1)
                    pe.wait_ge(S["xT_low"], i + 1)
                    pe.wait_ge(S["sil_ready"], i)
                    split_product(AC[0], XT, expert, 0, "h0_full")
                    pe.wait_ge(S["h_scaled"], i)
                    transpose_h()
                    split_product(AC[1], XT, expert, DC, "h1_full")
                    transpose_x(s, pair + 1)
                    pe.wait_ge(S["hT_low"], i)
                    pe.wait_ge(S["cw_ready"], i * 2)
                    split_product(RB[0], HT, before, 2 * DC, "y_full")
            last_expert = pe.value_load(slot_expert[0:1, SLOT_TILES - 1:SLOT_TILES], min_val=0, max_val=E - 1)
            pe.wait_ge(S["h_scaled"], SLOT_TILES)
            transpose_h()
            pe.wait_ge(S["hT_low"], SLOT_TILES)
            split_product(RB[0], HT, last_expert, 2 * DC, "y_full")

        @block.gpsimd
        def _(pool):
            G_ = nc.gpsimd
            values = Values()
            imprecise = dict(allow_small_or_imprecise_dtypes=True)
            G_.memset(ident[:], 0.0).then_inc(S["ident_zero"], 1)
            G_.memset(upper[:], 1.0).then_inc(S["ident_zero"], 1)
            G_.memset(ones[:], 1.0)
            G_.iota(iota_e[:], pattern=[[1, E]], base=0, channel_multiplier=0, **imprecise)
            G_.iota(iota_b[:], pattern=[[1, P]], base=0, channel_multiplier=0, **imprecise)
            G_.iota(iota_p[:], pattern=[[0, 1]], base=0, channel_multiplier=1, **imprecise)
            G_.iota(tidx[:], pattern=[[P, NT]], base=0, channel_multiplier=1, **imprecise)
            G_.iota(token16[:], pattern=[[P, 2]], base=0, channel_multiplier=1, **imprecise)
            pool.wait_ge(S["ident_zero"], 2)
            G_.affine_select(out=upper[:], in_=upper[:], compare_op=ALU.is_gt, fill=0.0, base=0,
                             pattern=[[1, P]], channel_multiplier=-1)
            G_.affine_select(out=ident[:], in_=ident[:], compare_op=ALU.not_equal, fill=1.0, base=0,
                             pattern=[[-1, P]], channel_multiplier=1).then_inc(S["consts_ready"], 1)

            def body(first, second):
                at = values.at
                one, two = first is not None, second is not None
                low = split_turns(low_part, pool, *split_share(first, second))
                low(2)
                if two:
                    pool.wait_ge(S["s2_row_ready"], at("s2_row_ready", 1))
                    for j in range(TJ):
                        G_.tensor_tensor(T2[:, j, :], W2[:, j, :], s2_row, ALU.mult).then_inc(S["w2_scaled"], 1)
                low(3)
                if one:
                    pool.wait_ge(S["s1_row_ready"], at("s1_row_ready", 1))
                    for j in range(TJ):
                        G_.tensor_tensor(T1[:, j, :], W1[:, j, :], s1_row, ALU.mult).then_inc(S["w1_scaled"], 1)
                low(2)
                if two:
                    pool.wait_ge(S["xr_in"], at("xr_in", 1))
                    for j in range(TJ):
                        pool.wait_ge(S["ac_free"], 2 + at("ac_free", j + 1))
                        G_.tensor_tensor(XR[:, j, :], XR[:, j, :], OT[:, j % 2, :], ALU.add).then_inc(S["x2_ready"], 1)
                low(2)
                if one:
                    for j in range(TJ):
                        pool.wait_ge(S["silu_ready"], at("silu_ready", j + 1))
                        G_.tensor_tensor(A[:, j, :], T1[:, 4 + j, 0:I], T1[:, j, I:2 * I],
                                         ALU.mult).then_inc(S["a_ready"], 1)
                low(2 * KC)

            steps(pool, body, values)

            def take(dst, at, n):
                G_.tensor_copy(dst, slot_token[:, bass.ds(at, 1)]).then_inc(S["p_chain"], 1)
                pool.wait_ge(S["p_chain"], n)
                pool.sem_inc(S["p_passed"], 1)

            def gather(s):
                G_.indirect_dma_start(out=G[:, s, :], out_offset=None, in_=rows,
                                      in_offset=bass.IndirectOffsetOnAxis(ap=idx_gather[:, s:s + 1], axis=0),
                                      ).then_inc(gathered[s], 16)

            def scatter():
                G_.indirect_dma_start(out=out_rows, in_=YS, in_offset=None, compute_op=ALU.add,
                                      out_offset=bass.IndirectOffsetOnAxis(ap=idx_scatter[:, 0:1], axis=0),
                                      ).then_inc(S["scattered"], 16)

            low = split_turns(low_part, pool, B + 2, 2 * KC)
            low(2 * KC)
            pool.wait_ge(S["cw_row_ready"], 1)
            pool.dma_start(rows_v[:, :, D:ROW], top[:]).then_inc(S["w_out_done"], 16)
            pool.wait_ge(S["slots_ready"], 1)
            pool.wait_ge(S["w_out_done"], 16)
            pool.wait_ge(S["rows_done"], 16 * B)
            pool.wait_ge(S["x_out_done"], 16 * B)
            for at in range(2):
                take(idx_gather[:, at:at + 1], at, at + 1)
                gather(at)
            pool.wait_ge(S["xT_full"], 1)
            pool.wait_ge(S["weight_taken"], 1)
            take(idx_gather[:, 0:1], 2, 3)
            gather(0)
            pool.sem_inc(S["ys_free"], 1)
            with pool.Fori(1, SLOT_TILES // 2 + 1) as pair:
                for s in range(2):
                    k = pair * 2 + s
                    take(idx_scatter[:], k - 2, k * 2)
                    pool.wait_ge(S["ys_ready"], k - 1)
                    pool.sem_inc(S["p_passed"], 1)
                    scatter()
                    pool.wait_ge(S["xT_full"], k)
                    pool.wait_ge(S["weight_taken"], k)
                    take(idx_gather[:, 1 - s:2 - s], k + 1, k * 2 + 1)
                    gather(1 - s)
                    pool.wait_ge(S["scattered"], (k - 1) * 16)
                    pool.sem_inc(S["ys_free"], 1)
            take(idx_scatter[:], SLOT_TILES - 1, SLOT_TILES * 2 + 2)
            pool.wait_ge(S["ys_ready"], SLOT_TILES)
            scatter()
            pool.wait_ge(S["scattered"], SLOT_TILES * 16)
            pool.wait_ge(gathered[0], (IDX_COLS + 1) // 2 * 16)
            pool.wait_ge(gathered[1], IDX_COLS // 2 * 16)


_INS = ["x", "fside_BxS2xS2_0", "ctx_1024", "g_xattn", "g_ffn", "L0_ffn_gate_kernel", "L0_ffn_wi_0", "L0_ffn_wi_1", "L0_ffn_wo"]


def kernel(**inputs):
    import numpy as np
    import concourse.bacc as bacc
    from concourse.bass_utils import run_bass_kernel_spmd

    nc = bacc.Bacc("TRN2", target_bir_lowering=False, num_devices=1, dynamic_dma_scratch_size=4096)
    arrays, args = {}, []
    for name in _INS:
        a = np.ascontiguousarray(inputs[name])
        arrays[f"in_{name}"] = a
        args.append(nc.dram_tensor(f"in_{name}", a.shape, mybir.dt.from_np(a.dtype), kind="ExternalInput").ap())
    args.append(nc.dram_tensor("out", (B, T, D), F32, kind="ExternalOutput").ap())
    program(nc, *args)
    return run_bass_kernel_spmd(nc, [arrays], core_ids=[0]).results[0]["out"]
```

```python
import concourse.bass as bass
from concourse import mybir
from concourse.alu_op_type import AluOpType as ALU
from contextlib import ExitStack

F32, BF16, F16 = mybir.dt.float32, mybir.dt.bfloat16, mybir.dt.float16
I32, U32 = mybir.dt.int32, mybir.dt.uint32
ACT = mybir.ActivationFunctionType
AX = mybir.AxisListType

P = 128
B, T, D = 4, 512, 512
I = 256
E, M, TOPK = 8, 512, 2
TJ = T // P
DC, IC, MC = D // P, I // P, M // P
NT = B * TJ
SLOT_TILES = B * T * TOPK // P + E - 1
IDX_COLS = SLOT_TILES + 3
ROW = D + E
EPS_Q, QMAX, EPS_LN = 1e-6, 127.0, 1e-5
MAGIC = 1.5 * 2.0 ** 23
KC = 3 * DC
KW = KC * M
LAST_LOWS = 3
LEAD_SPLITS = 8
RING = 4
SPLIT_SCALE = 2.0 ** 8
H_TOP = 2.0 ** 12


def program(nc, x, guw, dw, g_xattn, g_ffn, gate_kernel, wi_0, wi_1, wo, out):
    rows = nc.dram_tensor("token_rows", [B * T, ROW], F32, kind="Internal").ap()
    x_v = x.rearrange("b (j p) d -> b p j d", p=P)
    guw_v = guw.rearrange("b (r p) d -> b p r d", p=P)
    dw_v = dw.rearrange("b (r p) i -> b p r i", p=P)
    out_rows = out.rearrange("b t d -> (b t) d")
    out_v = out_rows.rearrange("(n p) d -> p n d", p=P)
    rows_v = rows.rearrange("(n p) c -> p n c", p=P)
    expert_v = [w.rearrange("e (c p) n -> e p c n", p=P) for w in (wi_0, wi_1, wo)]

    ctx = ExitStack()
    with ctx:
        def sb(name, shape, dt):
            return ctx.enter_context(nc.sbuf_tensor(name, shape, dt))

        def pb(name):
            return ctx.enter_context(nc.psum_tensor(name, [P, 512], F32))

        experts = sb("experts", [P, E, KC, 2, M], F16)
        flat = experts[:].rearrange("p e k h n -> p (e k h n)").bitcast(F32)
        LATE = 3
        cursor = [(E - LATE) * KW]

        def early(words):
            at = cursor[0]
            cursor[0] += words
            assert cursor[0] <= E * KW
            return flat[:, at:at + words]

        X1 = early(TJ * D).rearrange("p (j d) -> p j d", d=D)
        W1 = early(TJ * D).rearrange("p (r d) -> p r d", d=D)
        w1qT = early(DC * T // 2).bitcast(BF16).rearrange("p (c o) -> p c o", c=DC)
        xqT = early(DC * T // 2).bitcast(BF16).rearrange("p (c t) -> p c t", c=DC)
        T1 = early(8 * D).rearrange("p (k d) -> p k d", d=D)
        FREED = (cursor[0] - (E - LATE) * KW) // M
        XR = early(TJ * D).rearrange("p (j d) -> p j d", d=D)
        t2_words = early(8 * I)
        T2 = t2_words.rearrange("p (k i) -> p k i", i=I)
        XN2 = t2_words.rearrange("p (j d) -> p j d", d=D)
        A = early(TJ * I).rearrange("p (j i) -> p j i", i=I)
        W2 = early(TJ * I).rearrange("p (r i) -> p r i", i=I)
        xn2T = early(DC * T).rearrange("p (c t) -> p c t", c=DC)
        quantised = xn2T.rearrange("p c t -> p (c t)").bitcast(BF16)
        w2qT = quantised[:, 0:IC * T].rearrange("p (c o) -> p c o", c=IC)
        aqT = quantised[:, IC * T:2 * IC * T].rearrange("p (c t) -> p c t", c=IC)

        REGION = 3328
        region = sb("region", [P, REGION], F32)

        def part(at, words):
            assert at + words <= REGION
            return region[:, at:at + words]

        s1_row = part(0, D)
        s2_row = part(512, I)
        w1_scale_row = part(768, D)
        w2_scale_row = part(1280, D)
        OT = part(1792, 2 * D).rearrange("p (s d) -> p s d", s=2)
        logits_e = part(2816, T)
        onehot_b = part(0, 8 * P).bitcast(F16).rearrange("p (s n b) -> p s n b", s=2, b=P)
        onehot_u = part(0, E * P).bitcast(F16).rearrange("p (n b) -> p n b", b=P)
        onehot_a = part(8 * P, NT * IDX_COLS).bitcast(F16).rearrange("p (n a) -> p n a", a=IDX_COLS)
        RT = 8 * P + NT * IDX_COLS
        rt = [part(RT + P * k, P).rearrange("p (e n) -> p e n", e=E) for k in range(7)]
        slot_xy = part(RT + 2 * P, 6 * NT).rearrange("p (k n) -> p k n", k=3)
        slot_i = part(RT + 5 * P, 6 * NT).bitcast(I32).rearrange("p (k n) -> p k n", k=3)
        mask16 = part(RT + 7 * P, P // 2).bitcast(BF16).rearrange("p (n e) -> p n e", e=E)
        slot_work = part(RT + 3 * P, IDX_COLS * E).rearrange("p (n e) -> p n e", e=E)
        G = part(0, 2 * ROW).rearrange("p (s c) -> p s c", s=2)
        YS = part(2 * ROW, D)
        cwm = part(2 * ROW + D, E)
        cw_tile, hmax, hcap, hinv, cwy = (part(2 * ROW + D + E + k, 1) for k in range(5))

        ring = sb("ring", [P, RING, M], F32)
        XT = ring[:, 0, :].bitcast(F16).rearrange("p (h c s) -> p h c s", h=2, c=DC)
        HT = ring[:, 1, :].bitcast(F16).rearrange("p (h c s) -> p h c s", h=2, c=MC)
        SIL, HH = ring[:, 2, :], ring[:, 3, :]
        ident = sb("ident", [P, P], F32)
        upper = sb("upper", [P, P], BF16)
        ones = sb("ones", [P, P], BF16)
        gate_sb = sb("gate_sb", [P, DC, E], F32)
        bst = sb("bst", [P, 2, TJ, 6], F32)
        mv = sb("mv", [P, 2, TJ, 2], F32)
        var_eps = sb("var_eps", [P, 2, TJ], F32)
        sd = sb("sd", [P, 2, TJ], F32)
        rstd = sb("rstd", [P, 2, TJ], F32)
        shift = sb("shift", [P, 2, TJ], F32)
        amax = sb("amax", [P, 2, 2, 4], F32)
        amax_c = sb("amax_c", [P, 2, 2, 4], F32)
        amax_r = sb("amax_r", [P, 2, 4], F32)
        ratio = sb("ratio", [P, 2, 4], F32)
        smooth = sb("smooth", [P, 2, 2, 4], F32)
        rowmax = sb("rowmax", [P, 2, 2, 4], F32)
        qscale = sb("qscale", [P, 2, 2, 4], F32)
        qinv = sb("qinv", [P, 2, 2, 4], F32)
        gates = sb("gates", [P, 2], F32)
        tanh_g = sb("tanh_g", [P, 2], F32)
        logits = sb("logits", [P, TJ, E], F32)
        top = sb("top", [P, NT, 8], F32)
        choice = sb("choice", [P, NT, TOPK], F32)
        row_top = sb("row_top", [P, TJ, 8], F32)
        row_top_i = sb("row_top_i", [P, TJ, 8], U32)
        n_e = sb("n_e", [P, 4, E], F32)
        n_i = sb("n_i", [P, 2, E], I32)
        iota_e = sb("iota_e", [P, E], F32)
        spare_e = sb("spare_e", [P, E], F32)
        token16 = sb("token16", [P, 2], F16)
        iota_b = sb("iota_b", [P, P], F32)
        iota_p = sb("iota_p", [P, 1], F32)
        tidx = sb("tidx", [P, NT], F32)
        tm = sb("tm", [P, 5, IDX_COLS], F32)
        slot_expert = sb("slot_expert", [P, IDX_COLS], I32)
        slot_token = sb("slot_token", [P, IDX_COLS], I32)
        slot_onehot = sb("slot_onehot", [P, IDX_COLS, E], F32)
        idx_gather = sb("idx_gather", [P, 2], I32)
        idx_scatter = sb("idx_scatter", [P, 1], I32)

        TV = [pb(f"TV{k}") for k in range(2)]
        TA = [pb(f"TA{k}") for k in range(2)]
        RB = [pb(f"RB{k}") for k in range(2)]
        AC = [pb(f"AC{k}") for k in range(2)]

        counts = dict(
            x1_in=(1, 0, 0), w1_in=(1, 0, 0), w2_in=(0, 1, 0), xr_in=(0, 0, 1),
            x_out_done=(0, 0, 1), rows_done=(0, 0, 1),
            var1_ready=(1, 0, 0), sd1_ready=(1, 0, 0), norm1_ready=(1, 0, 0), xn1_ready=(TJ, 0, 0),
            var2_ready=(0, 0, 1), sd2_ready=(0, 0, 1), norm2_ready=(0, 0, 1), xn2_ready=(0, 0, TJ),
            tv_full=(2 * DC, IC, IC), tv_free=(2 * DC, IC, IC),
            ta_full=(0, 2 * DC, 2 * IC + TJ), ta_free=(0, 2 * DC, 2 * IC + TJ),
            ac_full=(0, TJ, TJ), ac_free=(0, TJ, TJ),
            ratio1_ready=(0, 1, 0), root1_ready=(0, 1, 0), smooth1_ready=(0, 1, 0),
            ratio2_ready=(0, 0, 1), root2_ready=(0, 0, 1), smooth2_ready=(0, 0, 1),
            s1_row_full=(0, 1, 0), s1_row_ready=(0, 1, 0), inv1_full=(0, 1, 0),
            rows2_full=(0, 0, 1), s2_row_ready=(0, 0, 1), w1_scaled=(0, TJ, 0), w2_scaled=(0, 0, TJ),
            qx_ready=(0, 1, 0), qw1_ready=(0, 1, 0), qa_ready=(0, 0, 1), qw2_ready=(0, 0, 1),
            magic1_ready=(0, 8, 0), magic2_ready=(0, 0, 8), scale1_full=(0, 1, 0), scale1_ready=(0, 1, 0),
            scale2_full=(0, 0, 1), scale2_ready=(0, 0, 1), silu_ready=(0, TJ, 0), a_ready=(0, TJ, 0),
            x2_ready=(0, 0, TJ), logits_full=(0, 0, 1), logits_sb=(0, 0, 1), logits_t_full=(0, 0, 1),
        )
        names = """high_ready low_ready ident_zero consts_ready gates_in gate_in tanh_ready w_out_done v_chain v_passed pe_passed
            exp_ready diff_ready cw_row_ready mask_ready counts_full onehot_ready
            onehot_u_ready spare_full onehot_used slots_ready p_chain p_passed
            weight_taken xT_full xT_high xT_low h0_full h1_full sil_ready hh_ready
            h_scaled hT_full hT_high hT_low y_full ys_ready ys_free cw_ready scattered""".split()
        S = {n: ctx.enter_context(nc.semaphore(n)) for n in list(counts) + names}
        gathered = [ctx.enter_context(nc.semaphore(f"gathered{s}")) for s in range(2)]
        chunk_in = [ctx.enter_context(nc.semaphore(f"chunk_in{k}")) for k in range(RING)]
        block = ctx.enter_context(nc.Block())

        DMA_UNIT = {n: 16 for n in ("x1_in", "w1_in", "w2_in", "xr_in", "x_out_done", "rows_done")}

        class Values:

            def enter(self, loop_step, whole):
                self.loop_step, self.whole = loop_step, whole

            def at(self, name, n):
                unit = DMA_UNIT.get(name, 1)
                before = unit * (sum(c * w for c, w in zip(counts[name], self.whole)) + n)
                if self.loop_step is None:
                    return before
                return self.loop_step * (unit * sum(counts[name])) + before

        def steps(engine, body, values):
            values.enter(None, (0, 0, 0))
            body(0, None, None)
            values.enter(None, (1, 0, 0))
            body(1, 0, None)
            with engine.Fori(0, B - 1) as b:
                values.enter(b, (2, 1, 0))
                body(b + 2, b + 1, b)
            values.enter(None, (B + 1, B, B - 1))
            body(None, None, B - 1)

        def cols(ap, n):
            return ap.unsqueeze(2).to_broadcast([P, ap.shape[1], n])

        @block.sync
        def _(sp):
            def chunk(e, k):
                sp.dma_start(ring[:, k % RING, :],
                             expert_v[k // DC][bass.ds(e, 1), :, k % DC, :].rearrange("a p n -> (a p) n")
                             ).then_inc(chunk_in[k % RING], 16)

            for k in range(RING):
                chunk(0, k)
            for k in range(RING, KC):
                sp.wait_ge(S["low_ready"], k - RING + 1)
                chunk(0, k)
            with sp.Fori(1, E) as e:
                for k in range(KC):
                    sp.wait_ge(S["low_ready"], e * KC + k - RING + 1)
                    chunk(e, k)

        def high_part(act, e, k):
            act.wait_ge(chunk_in[k % RING], e * (16 * KC // RING) + 16 * (k // RING + 1))
            nc.scalar.activation(experts[:, bass.ds(e, 1), k, 0, :].rearrange("p a n -> p (a n)"), ring[:, k % RING, :],
                                 ACT.Copy, scale=SPLIT_SCALE)
            nc.scalar.activation(ring[:, k % RING, :], ring[:, k % RING, :], ACT.Copy,
                                 scale=SPLIT_SCALE).then_inc(S["high_ready"], 1)

        def low_part(engine, e, k, compute=nc.gpsimd):
            engine.wait_ge(S["high_ready"], e * KC + k + 1)
            at = experts[:, bass.ds(e, 1), k, :, :].rearrange("p a h n -> p (a h) n")
            compute.tensor_tensor(at[:, 1, :], ring[:, k % RING, :], at[:, 0, :],
                                  ALU.subtract).then_inc(S["low_ready"], 1)

        def split_turns(emit, engine, e, chunks, done=0, interleave=True):
            done, chunks = [done], done + chunks

            def some(n=None):
                for _ in range(chunks - done[0] if n is None else min(n, chunks - done[0]) if interleave else 0):
                    emit(engine, e + done[0] // KC, done[0] % KC)
                    done[0] += 1
            return some

        def split_share(lead, first, second):
            if second is None:
                return (0, LEAD_SPLITS, 0, False) if first is None else (0, 2 * KC - LEAD_SPLITS, LEAD_SPLITS)
            return (B + 1, FREED) if first is None else (first + 1, KC)

        @block.vector
        def _(dve):
            V = nc.vector
            values = Values()
            chain = [0]
            CHAIN = (3, 8, 15)
            counts["v_chain"] = CHAIN

            def link(ins):
                chain[0] += 1
                ins.then_inc(S["v_chain"], 1)
                dve.wait_ge(S["v_chain"], values.at("v_chain", chain[0]))

            def gap():
                dve.sem_inc(S["v_passed"], 1)

            dve.sem_inc(S["tv_free"], 2)
            dve.sem_inc(S["ac_free"], 2)

            def body(lead, first, second):
                chain[0] = 0
                at = values.at
                ahead, one, two = (row is not None for row in (lead, first, second))
                ac = [0]

                def statistics(h, tile_of, ready):
                    gap()
                    for j in range(TJ):
                        last = V.bn_stats(bst[:, h, j, :], tile_of(j))
                    link(last)
                    gap()
                    for j in range(TJ):
                        last = V.bn_aggr(mv[:, h, j, :], bst[:, h, j, :])
                    link(last)
                    V.tensor_scalar(var_eps[:, h, :], mv[:, h, :, 1], EPS_LN, None, ALU.add).then_inc(S[ready], 1)

                def normaliser(h, sd_ready, ready):
                    dve.wait_ge(S[sd_ready], at(sd_ready, 1))
                    link(V.reciprocal(rstd[:, h, :], sd[:, h, :]))
                    V.scalar_tensor_tensor(shift[:, h, :], mv[:, h, :, 0], -1.0, rstd[:, h, :],
                                           ALU.mult, ALU.mult).then_inc(S[ready], 1)

                def column_maxima(h, which, chunks):
                    for c in chunks:
                        dve.wait_ge(S["tv_full"], at("tv_full", tv[0] + 1))
                        V.tensor_reduce(amax[:, h, which, c:c + 1], TV[tv[0] % 2][:], axis=AX.X,
                                        op=ALU.max, apply_absolute_value=True).then_inc(S["tv_free"], 1)
                        tv[0] += 1

                def smoothing_ratio(h, n, ready):
                    dve.wait_ge(S["tv_free"], 2 + at("tv_free", tv[0]))
                    link(V.tensor_scalar(amax_c[:, h, :, 0:n], amax[:, h, :, 0:n], EPS_Q, None, ALU.max))
                    link(V.reciprocal(amax_r[:, h, 0:n], amax_c[:, h, 0, 0:n]))
                    V.tensor_tensor(ratio[:, h, 0:n], amax_c[:, h, 1, 0:n], amax_r[:, h, 0:n],
                                    ALU.mult).then_inc(S[ready], 1)

                def smoothing(h, n, root_ready, ready):
                    dve.wait_ge(S[root_ready], at(root_ready, 1))
                    link(V.tensor_scalar(smooth[:, h, 0, 0:n], smooth[:, h, 0, 0:n], EPS_Q, None, ALU.max))
                    V.reciprocal(smooth[:, h, 1, 0:n], smooth[:, h, 0, 0:n]).then_inc(S[ready], 1)

                def row_scales(h, which, tiles, ready):
                    link(V.tensor_reduce(rowmax[:, h, which, :], tiles, axis=AX.X, op=ALU.max,
                                         apply_absolute_value=True))
                    link(V.tensor_scalar(qscale[:, h, which, :], rowmax[:, h, which, :], EPS_Q, 1.0 / QMAX,
                                         ALU.max, ALU.mult))
                    V.reciprocal(qinv[:, h, which, :], qscale[:, h, which, :]).then_inc(S[ready], 1)

                tv = [0]
                if two:
                    column_maxima(1, 1, range(IC))
                if one:
                    smoothing_ratio(0, DC, "ratio1_ready")
                if two:
                    smoothing_ratio(1, IC, "ratio2_ready")
                    smoothing(1, IC, "root2_ready", "smooth2_ready")
                if one:
                    smoothing(0, DC, "root1_ready", "smooth1_ready")
                if two:
                    dve.wait_ge(S["s2_row_ready"], at("s2_row_ready", 1))
                    for j in range(TJ):
                        last = V.tensor_tensor(T2[:, 4 + j, :], A[:, j, :], RB[1][:, I:2 * I], ALU.mult)
                    link(last)
                    row_scales(1, 1, T2[:, 4:8, :], "qa_ready")
                    dve.wait_ge(S["w2_scaled"], at("w2_scaled", TJ))
                    row_scales(1, 0, T2[:, 0:4, :], "qw2_ready")
                if one:
                    dve.wait_ge(S["inv1_full"], at("inv1_full", 1))
                    for j in range(TJ):
                        last = V.tensor_tensor(T1[:, 4 + j, :], X1[:, j, :], RB[0][:], ALU.mult)
                    link(last)
                    row_scales(0, 1, T1[:, 4:8, :], "qx_ready")
                    dve.wait_ge(S["w1_scaled"], at("w1_scaled", TJ))
                    row_scales(0, 0, T1[:, 0:4, :], "qw1_ready")
                if two:
                    dve.wait_ge(S["scale2_ready"], at("scale2_ready", 1))
                    for j in range(TJ):
                        dve.wait_ge(S["ac_full"], at("ac_full", ac[0] + 1))
                        if j >= 2:
                            dve.wait_ge(S["x2_ready"], at("x2_ready", j - 1))
                        V.scalar_tensor_tensor(OT[:, j % 2, :], AC[j % 2][:], qscale[:, 1, 1, j:j + 1],
                                               w2_scale_row, ALU.mult, ALU.mult).then_inc(S["ac_free"], 1)
                        ac[0] += 1
                if ahead:
                    dve.wait_ge(S["x1_in"], at("x1_in", 1))
                    statistics(0, lambda j: X1[:, j, :], "var1_ready")
                if one:
                    column_maxima(1, 0, range(IC))
                if two:
                    dve.wait_ge(S["x2_ready"], at("x2_ready", TJ))
                    statistics(1, lambda j: XR[:, j, :], "var2_ready")
                    normaliser(1, "sd2_ready", "norm2_ready")
                if ahead:
                    normaliser(0, "sd1_ready", "norm1_ready")
                if one:
                    dve.wait_ge(S["scale1_ready"], at("scale1_ready", 1))
                    for j in range(TJ):
                        dve.wait_ge(S["ac_full"], at("ac_full", ac[0] + 1))
                        V.scalar_tensor_tensor(T1[:, j, :], AC[j % 2][:], qscale[:, 0, 1, j:j + 1],
                                               w1_scale_row, ALU.mult, ALU.mult).then_inc(S["ac_free"], 1)
                        ac[0] += 1
                if ahead:
                    column_maxima(0, 0, range(DC))
                    column_maxima(0, 1, range(DC))
                if two:
                    dve.wait_ge(S["logits_t_full"], at("logits_t_full", 1))
                    link(V.tensor_copy(logits[:].rearrange("p j e -> p (j e)"), AC[1][:, 0:TJ * E]))
                    gap()
                    for j in range(TJ):
                        last = V.max(row_top[:, j, :], logits[:, j, :])
                    link(last)
                    gap()
                    for j in range(TJ):
                        last = V.max_index(row_top_i[:, j, :], row_top[:, j, :], logits[:, j, :])
                    link(last)
                    V.tensor_copy(top[:, bass.ds(second * TJ, TJ), :], row_top[:])
                    link(V.tensor_copy(choice[:, bass.ds(second * TJ, TJ), :], row_top_i[:, :, 0:2]))
                assert chain[0] == sum(c for c, here in zip(CHAIN, (ahead, one, two)) if here), chain[0]

            dve.wait_ge(S["consts_ready"], 1)
            steps(dve, body, values)
            dve.wait_ge(S["ac_free"], 2 + TJ * 2 * B)
            base = sum(CHAIN) * B + CHAIN[0]
            chain[0] = 0

            def link(ins):
                chain[0] += 1
                ins.then_inc(S["v_chain"], 1)
                dve.wait_ge(S["v_chain"], base + chain[0])

            oh = [rt[k].rearrange("p e n -> p (e n)").rearrange("p (n e) -> p n e", e=E) for k in range(2)]
            diff, prob1, prob2, den = (tm[:, k, 0:NT] for k in (1, 2, 3, 4))
            iota_ne = iota_e[:].unsqueeze(1).to_broadcast([P, NT, E])
            V.tensor_tensor(diff, top[:, :, 1], top[:, :, 0], ALU.subtract).then_inc(S["diff_ready"], 1)
            V.tensor_tensor(oh[0], iota_ne, choice[:, :, 0:1].to_broadcast([P, NT, E]), ALU.is_equal)
            link(V.tensor_tensor(oh[1], iota_ne, choice[:, :, 1:2].to_broadcast([P, NT, E]), ALU.is_equal))
            V.tensor_tensor(mask16, oh[0], oh[1], ALU.add).then_inc(S["mask_ready"], 1)
            dve.wait_ge(S["mask_ready"], 1)
            fl = lambda ap: ap.rearrange("p e n -> p (e n)")
            dve.wait_ge(S["counts_full"], 1)
            within, total = RB[0][:, 0:P].rearrange("p (e n) -> p e n", e=E), RB[1][:, 0:P]
            tot, run, before, rank = rt[3], rt[4], rt[5], rt[6]
            V.tensor_copy(fl(tot), total)
            link(V.memset(fl(rank), 1.0))
            link(V.tensor_tensor_scan(fl(run), fl(rank), fl(tot), 0.0, ALU.mult, ALU.add))
            link(V.tensor_tensor(fl(before), fl(run), fl(tot), ALU.subtract))
            V.tensor_tensor(n_e[:, 0, :], run[:, :, NT - 1], before[:, :, 0], ALU.subtract)
            link(V.tensor_tensor(rank, before, before[:, :, 0:1].to_broadcast([P, E, NT]), ALU.subtract))
            link(V.tensor_tensor(rank, within, rank, ALU.add))
            aside = slot_work[:, 0:2 * E, 0].rearrange("p (e n) -> p e n", n=2)
            link(V.tensor_tensor(aside, tidx[:, 0:2].unsqueeze(1).to_broadcast([P, E, 2]), rank[:, :, 0:2], ALU.subtract))
            link(V.scalar_tensor_tensor(aside, mask16[:, 0:2, :].rearrange("p n e -> p e n"), float(B * T), aside,
                                        ALU.mult, ALU.add))
            V.tensor_tensor(onehot_u, iota_b[:].unsqueeze(1).to_broadcast([P, 2 * E, P]),
                            cols(aside.rearrange("p e n -> p (e n)"), P), ALU.is_equal).then_inc(S["onehot_u_ready"], 1)
            tiles_e, tiles_run = n_e[:, 1, :], n_e[:, 2, :]
            link(V.tensor_scalar(n_e[:, 1, :], n_e[:, 0, :], float(P - 1), None, ALU.add))
            V.memset(n_e[:, 3, :], 1.0)
            link(V.tensor_copy(n_i[:, 0, :], n_e[:, 1, :]))
            link(V.tensor_scalar(n_i[:, 1, :], n_i[:, 0, :], 7, None, ALU.arith_shift_right))
            link(V.tensor_copy(tiles_e, n_i[:, 1, :]))
            link(V.tensor_tensor_scan(tiles_run, n_e[:, 3, :], tiles_e, 0.0, ALU.mult, ALU.add))
            link(V.tensor_tensor(n_e[:, 3, :], tiles_run, tiles_e, ALU.subtract))
            link(V.scalar_tensor_tensor(rank, cols(n_e[:, 3, :], NT), float(P), rank, ALU.mult, ALU.add))
            for k in range(2):
                last = V.tensor_tensor(rt[3 + k].rearrange("p e n -> p (e n)").rearrange("p (n e) -> p n e", e=E), oh[k],
                                rank.rearrange("p e n -> p n e"), ALU.mult)
            link(last)
            slot_kn = slot_xy[:, 0, :]
            for k in range(2):
                last = V.tensor_reduce(slot_xy[:, 0, k * NT:(k + 1) * NT],
                                       rt[3 + k].rearrange("p e n -> p (e n)").rearrange("p (n e) -> p n e", e=E),
                                       axis=AX.X, op=ALU.add)
            link(last)
            link(V.tensor_copy(slot_i[:, 0, :], slot_kn))
            V.tensor_scalar(slot_i[:, 1, :], slot_i[:, 0, :], 7, None, ALU.arith_shift_right)
            link(V.tensor_scalar(slot_i[:, 2, :], slot_i[:, 0, :], P - 1, None, ALU.bitwise_and))
            link(V.tensor_copy(slot_xy[:, 1:3, :], slot_i[:, 1:3, :]))
            link(V.tensor_tensor(onehot_a, iota_b[:, 0:IDX_COLS].unsqueeze(1).to_broadcast([P, 2 * NT, IDX_COLS]),
                                 cols(slot_xy[:, 1, :], IDX_COLS), ALU.is_equal))
            for k in range(2):
                V.tensor_tensor(onehot_a[:, k * NT:(k + 1) * NT], onehot_a[:, k * NT:(k + 1) * NT],
                                cols(tidx[:], IDX_COLS), ALU.mult)
            dve.wait_ge(S["spare_full"], 1)
            for t in range(4):
                at = slice(t * 8, t * 8 + 8)
                if t >= 2:
                    dve.wait_ge(S["onehot_used"], t - 1)
                V.tensor_tensor(onehot_b[:, t % 2], iota_b[:].unsqueeze(1).to_broadcast([P, 8, P]),
                                cols(slot_xy[:, 2, at], P), ALU.is_equal).then_inc(S["onehot_ready"], 1)
            dve.wait_ge(S["exp_ready"], 1)
            link(V.tensor_scalar(den, prob2, 1.0, None, ALU.add))
            link(V.reciprocal(prob1, den))
            link(V.tensor_tensor(prob2, prob2, prob1, ALU.mult))
            link(V.tensor_scalar(tm[:, 2:4, 0:NT], tm[:, 2:4, 0:NT], tanh_g[:, 1:2], None, ALU.mult))
            V.tensor_tensor(oh[0], oh[0], cols(prob1, E), ALU.mult)
            link(V.tensor_tensor(oh[1], oh[1], cols(prob2, E), ALU.mult))
            V.tensor_tensor(top[:], oh[0], oh[1], ALU.add).then_inc(S["cw_row_ready"], 1)
            iota_s = iota_b[:, 0:IDX_COLS]
            expert_of, first_of, count_of, pad_of, is_pad = (tm[:, k, :] for k in range(5))
            passed, product = slot_onehot[:], slot_work
            link(V.tensor_tensor(passed, cols(iota_s, E), tiles_run.unsqueeze(1).to_broadcast([P, IDX_COLS, E]), ALU.is_ge))
            V.tensor_reduce(expert_of, passed, axis=AX.X, op=ALU.add)
            link(V.tensor_tensor(product, passed, tiles_e.unsqueeze(1).to_broadcast([P, IDX_COLS, E]), ALU.mult))
            link(V.tensor_reduce(first_of, product, axis=AX.X, op=ALU.add))
            V.tensor_scalar(slot_expert[:], expert_of, float(E - 1), None, ALU.min)
            link(V.tensor_tensor(slot_onehot[:], iota_e[:].unsqueeze(1).to_broadcast([P, IDX_COLS, E]),
                                 cols(expert_of, E), ALU.is_equal))
            link(V.tensor_tensor(product, slot_onehot[:], n_e[:, 0, :].unsqueeze(1).to_broadcast([P, IDX_COLS, E]), ALU.mult))
            link(V.tensor_reduce(count_of, product, axis=AX.X, op=ALU.add))
            few, spare = n_e[:, 3, :], spare_e[:]
            V.tensor_scalar(few, n_e[:, 0, :], float(P), None, ALU.is_lt)
            link(V.tensor_scalar(spare, RB[1][:, P:P + E], iota_p[:, 0:1], None, ALU.subtract))
            link(V.tensor_tensor(spare, spare, few, ALU.mult))
            V.tensor_tensor(first_of, iota_s, first_of, ALU.subtract)
            link(V.tensor_tensor(product, slot_onehot[:], spare.unsqueeze(1).to_broadcast([P, IDX_COLS, E]), ALU.mult))
            V.tensor_reduce(pad_of, product, axis=AX.X, op=ALU.add)
            link(V.tensor_scalar(first_of, first_of, float(P), iota_p[:, 0:1], ALU.mult, ALU.add))
            link(V.tensor_tensor(is_pad, first_of, count_of, ALU.is_ge))
            link(V.tensor_scalar(pad_of, pad_of, iota_p[:, 0:1], None, ALU.add))
            V.tensor_tensor(first_of, first_of, count_of, ALU.is_lt)
            link(V.tensor_tensor(pad_of, pad_of, is_pad, ALU.mult))
            dve.wait_ge(S["onehot_used"], 4)
            V.tensor_tensor(slot_token[:], RB[0][:, 0:IDX_COLS], pad_of, ALU.add).then_inc(S["slots_ready"], 1)
            link(V.tensor_tensor(slot_onehot[:], slot_onehot[:], cols(first_of, E), ALU.mult))
            dve.wait_ge(S["low_ready"], E * KC - LAST_LOWS)
            for k in range(KC - LAST_LOWS, KC):
                low_part(dve, E - 1, k, nc.vector)

            def take_weights(at, s, turn):
                dve.wait_ge(gathered[s], turn * 16)
                V.tensor_tensor(cwm, G[:, s, D:ROW], slot_onehot[:, bass.ds(at, 1), :].rearrange("p a e -> p (a e)"),
                                ALU.mult).then_inc(S["weight_taken"], 1)

            def x_low(at):
                dve.wait_ge(S["xT_high"], at + 1)
                V.scalar_tensor_tensor(XT[:, 1].rearrange("p c s -> p (c s)"), TV[0][:], SPLIT_SCALE,
                                       XT[:, 0].rearrange("p c s -> p (c s)"), ALU.mult,
                                       ALU.subtract).then_inc(S["xT_low"], 1)

            def h_low(at):
                dve.wait_ge(S["hT_high"], at + 1)
                V.scalar_tensor_tensor(HT[:, 1].rearrange("p c s -> p (c s)"), TV[1][:], 1.0,
                                       HT[:, 0].rearrange("p c s -> p (c s)"), ALU.mult,
                                       ALU.subtract).then_inc(S["hT_low"], 1)

            def hidden(at):
                dve.wait_ge(S["sil_ready"], at + 1)
                dve.wait_ge(S["h1_full"], at + 1)
                V.tensor_tensor(HH, SIL, AC[1][:], ALU.mult).then_inc(S["hh_ready"], 1)
                dve.wait_ge(S["hh_ready"], at + 1)
                V.tensor_reduce(hmax, HH, axis=AX.X, op=ALU.max,
                                apply_absolute_value=True).then_inc(S["v_chain"], 1)
                dve.wait_ge(S["v_chain"], v0 + at * 3 + 1)
                V.tensor_scalar(hcap, hmax, 1e-30, 1.0 / H_TOP, ALU.max, ALU.mult).then_inc(S["v_chain"], 1)
                dve.wait_ge(S["v_chain"], v0 + at * 3 + 2)
                V.reciprocal(hinv, hcap).then_inc(S["v_chain"], 1)
                dve.wait_ge(S["v_chain"], v0 + at * 3 + 3)
                V.tensor_scalar(HH, HH, hinv, None, ALU.mult).then_inc(S["h_scaled"], 1)

            def output(n):
                dve.wait_ge(S["y_full"], n)
                dve.wait_ge(S["ys_free"], n)
                V.tensor_scalar(YS, RB[0][:], cwy, None, ALU.mult).then_inc(S["ys_ready"], 1)

            def weights(at):
                V.tensor_reduce(cw_tile, cwm, axis=AX.X, op=ALU.add).then_inc(S["cw_ready"], 1)
                dve.wait_ge(S["cw_ready"], at * 2 + 1)
                V.scalar_tensor_tensor(cwy, cw_tile, SPLIT_SCALE ** -3, hcap, ALU.mult,
                                       ALU.mult).then_inc(S["cw_ready"], 1)

            v0 = base + chain[0]
            take_weights(0, 0, 1)
            x_low(0)
            hidden(0)
            dve.wait_ge(S["weight_taken"], 1)
            weights(0)
            x_low(1)
            with dve.Fori(1, SLOT_TILES // 2 + 1) as pair:
                for s in range(2):
                    i = pair * 2 + (s - 1)
                    h_low(i - 1)
                    take_weights(i, 1 - s, pair + s)
                    dve.wait_ge(S["h1_full"], i + 1)
                    x_low(i + 1)
                    hidden(i)
                    output(i)
                    dve.wait_ge(S["ys_ready"], i)
                    weights(i)
            dve.sem_inc(S["weight_taken"], 1)
            h_low(SLOT_TILES - 1)
            dve.wait_ge(S["cw_ready"], 2 * SLOT_TILES)
            output(SLOT_TILES)

        @block.scalar
        def _(act):
            C = nc.scalar
            values = Values()

            def load(dst, src, row, sem):
                act.dma_start(dst, src[bass.ds(row, 1)].rearrange("a p j d -> (a p) j d")).then_inc(S[sem], 16)

            load(X1, x_v, 0, "x1_in")
            load(W1, guw_v, 0, "w1_in")
            act.dma_start(gates[:, 0:1], g_xattn.unsqueeze(0).to_broadcast([P, 1])).then_inc(S["gates_in"], 16)
            act.dma_start(gates[:, 1:2], g_ffn.unsqueeze(0).to_broadcast([P, 1])).then_inc(S["gates_in"], 16)
            act.dma_start(gate_sb[:], gate_kernel.rearrange("(c p) e -> p c e", p=P)).then_inc(S["gate_in"], 16)
            load(W2, dw_v, 0, "w2_in")
            load(XR, x_v, 0, "xr_in")
            act.sem_inc(S["ta_free"], 2)
            act.wait_ge(S["gates_in"], 32)
            C.activation(tanh_g[:], gates[:], ACT.Tanh).then_inc(S["tanh_ready"], 1)
            act.wait_ge(S["tanh_ready"], 1)

            def body(lead, first, second):
                at = values.at
                ahead, one, two = (row is not None for row in (lead, first, second))
                ta = [0]
                high = split_turns(high_part, act, *split_share(lead, first, second))

                def evacuate(dst, bias):
                    act.wait_ge(S["ta_full"], at("ta_full", ta[0] + 1))
                    bank = TA[ta[0] % 2][:]
                    if len(dst.shape) == 3:
                        bank = bank.rearrange("p (c t) -> p c t", c=dst.shape[1])
                    C.activation(dst, bank, ACT.Copy, bias=bias).then_inc(S["ta_free"], 1)
                    ta[0] += 1

                def deviations(h, wait, ready):
                    act.wait_ge(S[wait], at(wait, 1))
                    C.activation(sd[:, h, :], var_eps[:, h, :], ACT.Sqrt).then_inc(S[ready], 1)

                def smooth_root(h, n, wait, ready):
                    act.wait_ge(S[wait], at(wait, 1))
                    C.activation(smooth[:, h, 0, 0:n], ratio[:, h, 0:n], ACT.Sqrt).then_inc(S[ready], 1)

                def normalise(h, wait, src, dst, ready):
                    act.wait_ge(S[wait], at(wait, 1))
                    for j in range(TJ):
                        C.activation(dst[:, j, :], src[:, j, :], ACT.Identity, bias=shift[:, h, j:j + 1],
                                     scale=rstd[:, h, j:j + 1]).then_inc(S[ready], 1)

                def round_rows(h, which, tiles, wait, ready):
                    act.wait_ge(S[wait], at(wait, 1))
                    for j in range(TJ):
                        C.activation(tiles[:, j, :], tiles[:, j, :], ACT.Copy, bias=MAGIC,
                                     scale=qinv[:, h, which, j:j + 1]).then_inc(S[ready], 1)

                if two:
                    smooth_root(1, IC, "ratio2_ready", "root2_ready")
                if one:
                    smooth_root(0, DC, "ratio1_ready", "root1_ready")
                high(1)
                if two:
                    act.wait_ge(S["rows2_full"], at("rows2_full", 1))
                    C.activation(s2_row, RB[1][:, 0:I], ACT.Copy).then_inc(S["s2_row_ready"], 1)
                high(1)
                if one:
                    act.wait_ge(S["s1_row_full"], at("s1_row_full", 1))
                    C.activation(s1_row, RB[0][:], ACT.Copy).then_inc(S["s1_row_ready"], 1)
                high(2)
                if two:
                    round_rows(1, 1, T2[:, 4:8, :], "qa_ready", "magic2_ready")
                    for c in range(IC):
                        evacuate(aqT[:, c, :], -MAGIC)
                    round_rows(1, 0, T2[:, 0:4, :], "qw2_ready", "magic2_ready")
                    load(W2, dw_v, (second + 1) % B, "w2_in")
                high(3)
                if two:
                    for c in range(IC):
                        evacuate(w2qT[:, c, :], -MAGIC)
                    act.wait_ge(S["scale2_full"], at("scale2_full", 1))
                    C.activation(w2_scale_row, RB[1][:], ACT.Copy,
                                 scale=tanh_g[:, 0:1]).then_inc(S["scale2_ready"], 1)
                if not ahead:
                    high(1)
                if one:
                    round_rows(0, 1, T1[:, 4:8, :], "qx_ready", "magic1_ready")
                    load(X1, x_v, (first + 1) % B, "x1_in")
                    for c in range(0, 2):
                        evacuate(xqT[:, c, :], -MAGIC)
                if not ahead:
                    high(1)
                if one:
                    for c in range(2, DC):
                        evacuate(xqT[:, c, :], -MAGIC)
                if not ahead:
                    high(1)
                if one:
                    round_rows(0, 0, T1[:, 0:4, :], "qw1_ready", "magic1_ready")
                    load(W1, guw_v, (first + 1) % B, "w1_in")
                if not ahead:
                    high(1)
                if one:
                    for c in range(DC):
                        evacuate(w1qT[:, c, :], -MAGIC)
                high(1)
                if ahead:
                    deviations(0, "var1_ready", "sd1_ready")
                if one:
                    act.wait_ge(S["scale1_full"], at("scale1_full", 1))
                    C.activation(w1_scale_row, RB[0][:], ACT.Copy).then_inc(S["scale1_ready"], 1)
                if two:
                    deviations(1, "var2_ready", "sd2_ready")
                    act.dma_start(out_v[:, bass.ds(second * TJ, TJ), :], XR).then_inc(S["x_out_done"], 16)
                    normalise(1, "norm2_ready", XR, XN2, "xn2_ready")
                if not ahead:
                    high(1)
                if ahead:
                    normalise(0, "norm1_ready", X1, X1, "xn1_ready")
                if one:
                    for j in range(0, 2):
                        act.wait_ge(S["ac_free"], 2 + at("ac_free", (TJ if two else 0) + j + 1))
                        C.activation(T1[:, 4 + j, 0:I], T1[:, j, 0:I], ACT.Silu).then_inc(S["silu_ready"], 1)
                if two:
                    act.wait_ge(S["xn2_ready"], at("xn2_ready", TJ))
                    act.dma_start(rows_v[:, bass.ds(second * TJ, TJ), 0:D], XN2).then_inc(S["rows_done"], 16)
                    for j in range(TJ):
                        evacuate(xn2T[:, :, j * P:(j + 1) * P], 0.0)
                if one:
                    for j in range(2, TJ):
                        act.wait_ge(S["ac_free"], 2 + at("ac_free", (TJ if two else 0) + j + 1))
                        C.activation(T1[:, 4 + j, 0:I], T1[:, j, 0:I], ACT.Silu).then_inc(S["silu_ready"], 1)
                if not ahead:
                    high(4)
                if two:
                    act.wait_ge(S["logits_full"], at("logits_full", 1))
                    C.activation(logits_e[0:E, :], AC[0][0:E, :], ACT.Copy).then_inc(S["logits_sb"], 1)
                if not ahead:
                    high(1)
                if not ahead:
                    act.wait_ge(S["x1_in"], 16 * (B + 1))
                    act.wait_ge(S["w1_in"], 16 * (B + 1))
                    act.wait_ge(S["tv_free"], 2 + at("tv_free", 0))
                high()
                if two:
                    act.wait_ge(S["x_out_done"], at("x_out_done", 1))
                    load(XR, x_v, (second + 1) % B, "xr_in")
                    act.wait_ge(S["rows_done"], at("rows_done", 1))

            steps(act, body, values)
            act.wait_ge(S["diff_ready"], 1)
            C.activation(tm[:, 3, 0:NT], tm[:, 1, 0:NT], ACT.Exp).then_inc(S["exp_ready"], 1)
            act.wait_ge(S["ac_free"], 2 + 2 * TJ * B)
            act.wait_ge(S["w2_in"], 16 * (B + 1))
            act.wait_ge(S["xr_in"], 16 * (B + 1))
            high = split_turns(high_part, act, B + 1, 3 * KC - FREED, FREED)
            high(10)
            act.wait_ge(S["cw_row_ready"], 1)
            act.dma_start(rows_v[:, :, D:ROW], top[:]).then_inc(S["w_out_done"], 16)
            high()

            def x_high(at):
                act.wait_ge(S["xT_full"], at + 1)
                C.activation(XT[:, 0].rearrange("p c s -> p (c s)"), TV[0][:], ACT.Copy,
                             scale=SPLIT_SCALE).then_inc(S["xT_high"], 1)

            def silu(at):
                act.wait_ge(S["h0_full"], at + 1)
                C.activation(SIL, AC[0][:], ACT.Silu, scale=SPLIT_SCALE ** -2).then_inc(S["sil_ready"], 1)

            def h_high(at):
                act.wait_ge(S["hT_full"], at + 1)
                C.activation(HT[:, 0].rearrange("p c s -> p (c s)"), TV[1][:], ACT.Copy).then_inc(S["hT_high"], 1)

            act.wait_ge(S["low_ready"], KC * E)
            x_high(0)
            silu(0)
            act.wait_ge(S["h1_full"], 1)
            x_high(1)
            with act.Fori(1, SLOT_TILES) as i:
                h_high(i - 1)
                silu(i)
                act.wait_ge(S["h1_full"], i + 1)
                x_high(i + 1)
            h_high(SLOT_TILES - 1)

        @block.tensor
        def _(pe):
            T_ = nc.tensor
            values = Values()
            pe.wait_ge(S["consts_ready"], 1)
            pe.wait_ge(S["gate_in"], 16)

            def body(lead, first, second):
                at = values.at
                ahead, one, two = (row is not None for row in (lead, first, second))
                tv, ta, ac = [0], [0], [0]

                def transposes(k, banks, full, free, tiles):
                    pe.wait_ge(S[free], 1 + at(free, k[0]))
                    for n, t in enumerate(tiles):
                        last = T_.transpose(banks[k[0] % 2][:, n * P:(n + 1) * P], t, ident[:])
                    last.then_inc(S[full], 1)
                    k[0] += 1

                def to_vector(tiles):
                    transposes(tv, TV, "tv_full", "tv_free", tiles)

                def to_scalar(tiles):
                    transposes(ta, TA, "ta_full", "ta_free", tiles)

                def chunks(tiles, n):
                    return [[tiles[:, j, c * P:(c + 1) * P] for j in range(TJ)] for c in range(n)]

                def spread(bank, at_col, col, n):
                    for c in range(n):
                        last = T_.matmul(bank[:, at_col + c * P:at_col + (c + 1) * P],
                                         col[:, c:c + 1].to_broadcast([P, P]), ident[:], start=True, stop=True)
                    return last

                def product(aT, wT, n):
                    for j in range(TJ):
                        pe.wait_ge(S["ac_free"], 1 + at("ac_free", ac[0]))
                        for c in range(n):
                            last = T_.matmul(AC[j % 2][:], aT[:, c, j * P:(j + 1) * P], wT[:, c, :],
                                             start=(c == 0), stop=(c == n - 1))
                        last.then_inc(S["ac_full"], 1)
                        ac[0] += 1

                if two:
                    pe.wait_ge(S["a_ready"], at("a_ready", 0))
                    for tiles in chunks(A, IC):
                        to_vector(tiles)
                    pe.wait_ge(S["smooth2_ready"], at("smooth2_ready", 1))
                    spread(RB[1], 0, smooth[:, 1, 0, :], IC)
                    spread(RB[1], I, smooth[:, 1, 1, :], IC).then_inc(S["rows2_full"], 1)
                if one:
                    pe.wait_ge(S["smooth1_ready"], at("smooth1_ready", 1))
                    spread(RB[0], 0, smooth[:, 0, 0, :], DC).then_inc(S["s1_row_full"], 1)
                    pe.wait_ge(S["s1_row_ready"], at("s1_row_ready", 1))
                    spread(RB[0], 0, smooth[:, 0, 1, :], DC).then_inc(S["inv1_full"], 1)
                if two:
                    pe.wait_ge(S["magic2_ready"], at("magic2_ready", TJ))
                    for tiles in chunks(T2[:, 4:8, :], IC):
                        to_scalar(tiles)
                    pe.wait_ge(S["magic2_ready"], at("magic2_ready", 8))
                    for tiles in chunks(T2[:, 0:4, :], IC):
                        to_scalar(tiles)
                    spread(RB[1], 0, qscale[:, 1, 0, :], TJ).then_inc(S["scale2_full"], 1)
                    pe.wait_ge(S["ta_free"], 2 + at("ta_free", ta[0]))
                    product(aqT, w2qT, IC)
                if one:
                    pe.wait_ge(S["magic1_ready"], at("magic1_ready", TJ))
                    for tiles in chunks(T1[:, 4:8, :], DC):
                        to_scalar(tiles)
                    pe.wait_ge(S["w2_in"], at("w2_in", 1))
                    for tiles in chunks(W2, IC):
                        to_vector(tiles)
                    pe.wait_ge(S["magic1_ready"], at("magic1_ready", 8))
                    for tiles in chunks(T1[:, 0:4, :], DC):
                        to_scalar(tiles)
                    spread(RB[0], 0, qscale[:, 0, 0, :], TJ).then_inc(S["scale1_full"], 1)
                    pe.wait_ge(S["ta_free"], 2 + at("ta_free", ta[0]))
                    product(xqT, w1qT, DC)
                if ahead:
                    pe.wait_ge(S["w1_in"], at("w1_in", 1))
                    for tiles in chunks(W1, DC):
                        to_vector(tiles)
                    pe.wait_ge(S["xn1_ready"], at("xn1_ready", TJ))
                    for tiles in chunks(X1, DC)[0:2]:
                        to_vector(tiles)
                if two:
                    for j in range(TJ):
                        pe.wait_ge(S["xn2_ready"], at("xn2_ready", j + 1))
                        to_scalar([XN2[:, j, c * P:(c + 1) * P] for c in range(DC)])
                if ahead:
                    for tiles in chunks(X1, DC)[2:]:
                        to_vector(tiles)
                if two:
                    pe.wait_ge(S["ta_free"], 2 + at("ta_free", ta[0]))
                    pe.wait_ge(S["ac_free"], 2 + at("ac_free", ac[0]))
                    for c in range(DC):
                        last = T_.matmul(AC[0][0:E, :], gate_sb[:, c, :], xn2T[:, c, :],
                                         start=(c == 0), stop=(c == DC - 1))
                    last.then_inc(S["logits_full"], 1)
                    pe.wait_ge(S["logits_sb"], at("logits_sb", 1))
                    pe.sem_inc(S["pe_passed"], 1)
                    for j in range(TJ):
                        last = T_.transpose(AC[1][:, j * E:(j + 1) * E], logits_e[0:E, j * P:(j + 1) * P],
                                            ident[0:E, 0:E])
                    last.then_inc(S["logits_t_full"], 1)

            steps(pe, body, values)

            pe.wait_ge(S["mask_ready"], 1)
            mask_en = mask16.rearrange("p n e -> p e n")
            T_.matmul(RB[0][:, 0:P], upper[:], mask_en, start=True, stop=True)
            T_.matmul(RB[1][:, 0:P], ones[:], mask_en, start=True, stop=True).then_inc(S["counts_full"], 1)
            pe.wait_ge(S["onehot_u_ready"], 1)
            for e in range(E):
                for n in range(2):
                    last = T_.matmul(RB[1][:, P + e:P + e + 1], onehot_u[:, e * 2 + n, :], token16[:, n:n + 1],
                                     start=(n == 0), stop=(n == 1))
            last.then_inc(S["spare_full"], 1)
            for t in range(4):
                pe.wait_ge(S["onehot_ready"], t + 1)
                for n in range(t * 8, t * 8 + 8):
                    last = T_.matmul(RB[0][:, 0:IDX_COLS], onehot_b[:, t % 2, n % 8, :], onehot_a[:, n, :],
                                     start=(n == 0), stop=(n == 2 * NT - 1))
                last.then_inc(S["onehot_used"], 1)

            def transpose_x(s, turn):
                pe.wait_ge(gathered[s], turn * 16)
                for c in range(DC):
                    last = T_.transpose(TV[0][:, c * P:(c + 1) * P], G[:, s, c * P:(c + 1) * P], ident[:])
                last.then_inc(S["xT_full"], 1)

            def transpose_h():
                for c in range(MC):
                    last = T_.transpose(TV[1][:, c * P:(c + 1) * P], HH[:, c * P:(c + 1) * P], ident[:])
                last.then_inc(S["hT_full"], 1)

            def split_product(bank, act_T, expert, k0, full):
                for c in range(DC):
                    w = experts[:, bass.ds(expert, 1), k0 + c, :, :].rearrange("p a h n -> p (a h) n")
                    for n, (ah, wh) in enumerate(((0, 0), (0, 1), (1, 0))):
                        last = T_.matmul(bank[:], act_T[:, ah, c, :], w[:, wh, :],
                                         start=(c == 0 and n == 0), stop=(c == DC - 1 and n == 2))
                last.then_inc(S[full], 1)

            pe.wait_ge(S["slots_ready"], 1)
            first = pe.value_load(slot_expert[0:1, 0:1], min_val=0, max_val=E - 1)
            transpose_x(0, 1)
            pe.wait_ge(S["low_ready"], KC * E)
            pe.wait_ge(S["xT_low"], 1)
            split_product(AC[0], XT, first, 0, "h0_full")
            split_product(AC[1], XT, first, DC, "h1_full")
            transpose_x(1, 1)
            with pe.Fori(1, SLOT_TILES // 2 + 1) as pair:
                for s in range(2):
                    i = pair * 2 + (s - 1)
                    expert = pe.value_load(slot_expert[0:1, bass.ds(i, 1)], min_val=0, max_val=E - 1)
                    before = pe.value_load(slot_expert[0:1, bass.ds(i - 1, 1)], min_val=0, max_val=E - 1)
                    pe.wait_ge(S["xT_low"], i + 1)
                    pe.wait_ge(S["sil_ready"], i)
                    split_product(AC[0], XT, expert, 0, "h0_full")
                    pe.wait_ge(S["h_scaled"], i)
                    transpose_h()
                    split_product(AC[1], XT, expert, DC, "h1_full")
                    transpose_x(s, pair + 1)
                    pe.wait_ge(S["hT_low"], i)
                    pe.wait_ge(S["cw_ready"], i * 2)
                    split_product(RB[0], HT, before, 2 * DC, "y_full")
            last_expert = pe.value_load(slot_expert[0:1, SLOT_TILES - 1:SLOT_TILES], min_val=0, max_val=E - 1)
            pe.wait_ge(S["h_scaled"], SLOT_TILES)
            transpose_h()
            pe.wait_ge(S["hT_low"], SLOT_TILES)
            split_product(RB[0], HT, last_expert, 2 * DC, "y_full")

        @block.gpsimd
        def _(pool):
            G_ = nc.gpsimd
            values = Values()
            imprecise = dict(allow_small_or_imprecise_dtypes=True)
            G_.memset(ident[:], 0.0).then_inc(S["ident_zero"], 1)
            G_.memset(upper[:], 1.0).then_inc(S["ident_zero"], 1)
            G_.memset(ones[:], 1.0)
            G_.iota(iota_e[:], pattern=[[1, E]], base=0, channel_multiplier=0, **imprecise)
            G_.iota(iota_b[:], pattern=[[1, P]], base=0, channel_multiplier=0, **imprecise)
            G_.iota(iota_p[:], pattern=[[0, 1]], base=0, channel_multiplier=1, **imprecise)
            G_.iota(tidx[:], pattern=[[P, NT]], base=0, channel_multiplier=1, **imprecise)
            G_.iota(token16[:], pattern=[[P, 2]], base=0, channel_multiplier=1, **imprecise)
            pool.wait_ge(S["ident_zero"], 2)
            G_.affine_select(out=upper[:], in_=upper[:], compare_op=ALU.is_gt, fill=0.0, base=0,
                             pattern=[[1, P]], channel_multiplier=-1)
            G_.affine_select(out=ident[:], in_=ident[:], compare_op=ALU.not_equal, fill=1.0, base=0,
                             pattern=[[-1, P]], channel_multiplier=1).then_inc(S["consts_ready"], 1)

            def body(lead, first, second):
                at = values.at
                ahead, one, two = (row is not None for row in (lead, first, second))
                low = split_turns(low_part, pool, *split_share(lead, first, second))
                if two:
                    pool.wait_ge(S["s2_row_ready"], at("s2_row_ready", 1))
                    for j in range(TJ):
                        G_.tensor_tensor(T2[:, j, :], W2[:, j, :], s2_row, ALU.mult).then_inc(S["w2_scaled"], 1)
                low(3)
                if one:
                    pool.wait_ge(S["s1_row_ready"], at("s1_row_ready", 1))
                    for j in range(TJ):
                        G_.tensor_tensor(T1[:, j, :], W1[:, j, :], s1_row, ALU.mult).then_inc(S["w1_scaled"], 1)
                low(4)
                if not ahead:
                    low(1)
                if two:
                    pool.wait_ge(S["xr_in"], at("xr_in", 1))
                    for j in range(TJ):
                        pool.wait_ge(S["ac_free"], 2 + at("ac_free", j + 1))
                        G_.tensor_tensor(XR[:, j, :], XR[:, j, :], OT[:, j % 2, :], ALU.add).then_inc(S["x2_ready"], 1)
                if not ahead:
                    low(5)
                low(1)
                if not ahead:
                    low(1)
                if one:
                    for j in range(TJ):
                        pool.wait_ge(S["silu_ready"], at("silu_ready", j + 1))
                        G_.tensor_tensor(A[:, j, :], T1[:, 4 + j, 0:I], T1[:, j, I:2 * I],
                                         ALU.mult).then_inc(S["a_ready"], 1)
                if not ahead:
                    low(3)
                low()

            steps(pool, body, values)

            def take(dst, at, n):
                G_.tensor_copy(dst, slot_token[:, bass.ds(at, 1)]).then_inc(S["p_chain"], 1)
                pool.wait_ge(S["p_chain"], n)
                pool.sem_inc(S["p_passed"], 1)

            def gather(s):
                G_.indirect_dma_start(out=G[:, s, :], out_offset=None, in_=rows,
                                      in_offset=bass.IndirectOffsetOnAxis(ap=idx_gather[:, s:s + 1], axis=0),
                                      ).then_inc(gathered[s], 16)

            def scatter():
                G_.indirect_dma_start(out=out_rows, in_=YS, in_offset=None, compute_op=ALU.add,
                                      out_offset=bass.IndirectOffsetOnAxis(ap=idx_scatter[:, 0:1], axis=0),
                                      ).then_inc(S["scattered"], 16)

            low = split_turns(low_part, pool, B + 1, 3 * KC - FREED, FREED)
            low(3 * KC - FREED - LAST_LOWS)
            pool.wait_ge(S["slots_ready"], 1)
            pool.wait_ge(S["w_out_done"], 16)
            pool.wait_ge(S["rows_done"], 16 * B)
            pool.wait_ge(S["x_out_done"], 16 * B)
            for at in range(2):
                take(idx_gather[:, at:at + 1], at, at + 1)
                gather(at)
            for at in range(2, 4):
                pool.wait_ge(S["xT_full"], at - 1)
                pool.wait_ge(S["weight_taken"], at - 1)
                take(idx_gather[:, at - 2:at - 1], at, at + 1)
                gather(at - 2)
            pool.sem_inc(S["ys_free"], 1)
            with pool.Fori(1, SLOT_TILES // 2 + 1) as pair:
                for s in range(2):
                    k = pair * 2 + s
                    take(idx_scatter[:], k - 2, k * 2 + 1)
                    pool.wait_ge(S["ys_ready"], k - 1)
                    pool.sem_inc(S["p_passed"], 1)
                    scatter()
                    pool.wait_ge(S["xT_full"], k + 1)
                    pool.wait_ge(S["weight_taken"], k + 1)
                    take(idx_gather[:, s:s + 1], k + 2, k * 2 + 2)
                    gather(s)
                    pool.wait_ge(S["scattered"], (k - 1) * 16)
                    pool.sem_inc(S["ys_free"], 1)
            take(idx_scatter[:], SLOT_TILES - 1, SLOT_TILES * 2 + 3)
            pool.wait_ge(S["ys_ready"], SLOT_TILES)
            scatter()
            pool.wait_ge(S["scattered"], SLOT_TILES * 16)
            pool.wait_ge(gathered[0], (IDX_COLS + 1) // 2 * 16)
            pool.wait_ge(gathered[1], IDX_COLS // 2 * 16)


_INS = ["x", "fside_BxS2xS2_0", "ctx_1024", "g_xattn", "g_ffn", "L0_ffn_gate_kernel", "L0_ffn_wi_0", "L0_ffn_wi_1", "L0_ffn_wo"]


def kernel(**inputs):
    import numpy as np
    import concourse.bacc as bacc
    from concourse.bass_utils import run_bass_kernel_spmd

    nc = bacc.Bacc("TRN2", target_bir_lowering=False, num_devices=1, dynamic_dma_scratch_size=4096)
    arrays, args = {}, []
    for name in _INS:
        a = np.ascontiguousarray(inputs[name])
        arrays[f"in_{name}"] = a
        args.append(nc.dram_tensor(f"in_{name}", a.shape, mybir.dt.from_np(a.dtype), kind="ExternalInput").ap())
    args.append(nc.dram_tensor("out", (B, T, D), F32, kind="ExternalOutput").ap())
    program(nc, *args)
    return run_bass_kernel_spmd(nc, [arrays], core_ids=[0]).results[0]["out"]
```
